# Optimizing a Trainium2 kernel written in Bass

```python
import numpy as np
import jax
import jax.numpy as jnp

def _softmax(x, axis=-1):
    return jax.nn.softmax(x, axis=axis)

def _gelu(x):
    return jax.nn.gelu(x, approximate=True)

def _silu(x):
    return jax.nn.silu(x)

def _sigmoid(x):
    return jax.nn.sigmoid(x)

def _layernorm(x, axis=-1, eps=1e-05):
    m = jnp.mean(x, axis=axis, keepdims=True)
    v = jnp.var(x, axis=axis, keepdims=True)
    return (x - m) / jnp.sqrt(v + eps)

def _scatter_add(tgt, idx, src, axis=0):
    return tgt.at[idx].add(src)

def _segment_sum(src, seg, n):
    return jax.ops.segment_sum(src, seg, n)
kernel_name = 'mk_adaln_d1_jaxref_r4_1bcd97'

def setup_inputs(seed: int=0):
    np.random.seed(seed)
    _w = jnp.asarray

    def _L0_attn_setup():
        import jax, jax.numpy as jnp
        import numpy as np
        B, T, K, H = (2, 512, 256, 16)
        key = jax.random.key(seed)
        ks = jax.random.split(key, 9)
        sc = 0.02
        return {'x': jax.random.normal(ks[0], (B, T, K), dtype=jnp.float32), 'Wq_w': jax.random.normal(ks[1], (K, K), dtype=jnp.float32) * sc, 'Wq_b': jax.random.normal(ks[2], (K,), dtype=jnp.float32) * sc, 'Wk_w': jax.random.normal(ks[3], (K, K), dtype=jnp.float32) * sc, 'Wk_b': jax.random.normal(ks[4], (K,), dtype=jnp.float32) * sc, 'Wv_w': jax.random.normal(ks[5], (K, K), dtype=jnp.float32) * sc, 'Wv_b': jax.random.normal(ks[6], (K,), dtype=jnp.float32) * sc, 'Wo_w': jax.random.normal(ks[7], (K, K), dtype=jnp.float32) * sc, 'Wo_b': jax.random.normal(ks[8], (K,), dtype=jnp.float32) * sc}
    _L0_attn_in = _L0_attn_setup()

    def _L0_ffn_setup():
        import jax, jax.numpy as jnp
        import numpy as np
        E = 8
        K = 2
        D = 256
        B, N = (4, 1024)
        DC = 128
        key = jax.random.key(seed)
        ks = jax.random.split(key, 6)
        x = jax.random.normal(ks[0], (B, N, D), jnp.float32)
        cond = jax.random.normal(ks[1], (B, N, DC), jnp.float32)
        mask = jnp.ones((B, N), jnp.float32)
        W_shared = jax.random.normal(ks[2], (D, D), jnp.float32) * 0.02
        W_expert = jax.random.normal(ks[3], (D, D), jnp.float32) * 0.02
        W_gate = jax.random.normal(ks[4], (D, E - 1), jnp.float32) * 0.02
        bias = jnp.zeros((D,), jnp.float32)
        return dict(x=x, cond=cond, mask=mask, W_shared=W_shared, W_expert=W_expert, W_gate=W_gate, bias=bias)
    _L0_ffn_in = _L0_ffn_setup()
    _L0_c = _w((lambda *s: np.random.randn(*s).astype(np.float32) * 0.05)(4, 256))
    _L0_wmod = _w((lambda *s: np.random.randn(*s).astype(np.float32) * 0.05)(256, 6 * 256) * 256 ** (-0.5))
    _d = {'L0_attn_x': _L0_attn_in['x'], 'L0_attn_Wq_w': _L0_attn_in['Wq_w'], 'L0_attn_Wq_b': _L0_attn_in['Wq_b'], 'L0_attn_Wk_w': _L0_attn_in['Wk_w'], 'L0_attn_Wk_b': _L0_attn_in['Wk_b'], 'L0_attn_Wv_w': _L0_attn_in['Wv_w'], 'L0_attn_Wv_b': _L0_attn_in['Wv_b'], 'L0_attn_Wo_w': _L0_attn_in['Wo_w'], 'L0_attn_Wo_b': _L0_attn_in['Wo_b'], 'L0_ffn_cond': _L0_ffn_in['cond'], 'L0_ffn_mask': _L0_ffn_in['mask'], 'L0_ffn_W_shared': _L0_ffn_in['W_shared'], 'L0_ffn_W_expert': _L0_ffn_in['W_expert'], 'L0_ffn_W_gate': _L0_ffn_in['W_gate'], 'L0_ffn_bias': _L0_ffn_in['bias'], 'L0_c': _L0_c, 'L0_wmod': _L0_wmod}
    _x0 = _d['L0_attn_x']
    _d['L0_attn_x'] = jax.random.normal(jax.random.fold_in(jax.random.key(seed), 1), (4, 1024, 256), dtype=_x0.dtype)
    del _x0
    return _d

def reference(L0_attn_x, L0_attn_Wq_w, L0_attn_Wq_b, L0_attn_Wk_w, L0_attn_Wk_b, L0_attn_Wv_w, L0_attn_Wv_b, L0_attn_Wo_w, L0_attn_Wo_b, L0_ffn_cond, L0_ffn_mask, L0_ffn_W_shared, L0_ffn_W_expert, L0_ffn_W_gate, L0_ffn_bias, L0_c, L0_wmod):

    def _L0_attn_ref(x, Wq_w, Wq_b, Wk_w, Wk_b, Wv_w, Wv_b, Wo_w, Wo_b):
        import jax, jax.numpy as jnp
        import numpy as np
        B, T, K, H = (2, 512, 256, 16)
        b, t, k = x.shape
        h = H
        s = k // h
        q = x @ Wq_w.T + Wq_b
        kk = x @ Wk_w.T + Wk_b
        v = x @ Wv_w.T + Wv_b
        q = q.reshape(b, t, h, s).transpose(0, 2, 1, 3)
        kk = kk.reshape(b, t, h, s).transpose(0, 2, 1, 3)
        v = v.reshape(b, t, h, s).transpose(0, 2, 1, 3)
        dot = jnp.einsum('bhqd,bhkd->bhqk', q, kk)
        causal = jnp.tril(jnp.ones((t, t), dtype=bool))
        dot = jnp.where(causal, dot, -jnp.inf)
        dot = dot / jnp.sqrt(jnp.asarray(k, dot.dtype))
        attn = jax.nn.softmax(dot, axis=-1)
        out = jnp.einsum('bhqk,bhkd->bhqd', attn, v)
        out = out.transpose(0, 2, 1, 3).reshape(b, t, k)
        return out @ Wo_w.T + Wo_b

    def _L0_ffn_ref(x, cond, mask, W_shared, W_expert, W_gate, bias):
        import jax, jax.numpy as jnp
        import numpy as np
        E = 8
        K = 2
        D = 256
        B, N = (4, 1024)
        DC = 128
        b, n, d = x.shape
        T = b * n
        xf = x.reshape(T, d)
        scores = jax.nn.softmax(xf @ W_gate, axis=-1)
        expert_weights, _ = jax.lax.top_k(scores, K)
        expert_weights = expert_weights / expert_weights.sum(-1, keepdims=True)
        expert_indices = (jnp.arange(T * K) % E).reshape(T, K)
        te = expert_indices.reshape(-1)
        w = expert_weights.reshape(-1)
        capacity = K * T // E
        order = jnp.argsort(te, stable=True)
        sorted_e = te[order]
        hist = jnp.bincount(te, length=E)
        starts = jnp.concatenate([jnp.zeros((1,), hist.dtype), jnp.cumsum(hist)[:-1]])
        pos = jnp.arange(T * K) - starts[sorted_e]
        valid = pos < capacity
        dest = jnp.where(valid, sorted_e * capacity + pos, E * capacity)
        tok = order // K
        gathered = jnp.zeros((E * capacity + 1, d), x.dtype).at[dest].set(xf[tok])
        gathered = gathered[:-1]
        y = gathered @ W_expert.T
        contrib = w[order][:, None] * y[jnp.minimum(dest, E * capacity - 1)]
        moe_out = jnp.zeros((T, d), x.dtype).at[tok].add(jnp.where(valid[:, None], contrib, 0.0))
        shared = xf @ W_shared.T
        out = (shared + moe_out + bias).reshape(b, n, d)
        return out
    x = L0_attn_x
    mod = (_silu(L0_c) @ L0_wmod).reshape(L0_c.shape[0], 6, 1, -1)
    sa, ca, ga, sb, cb, gb = (mod[:, 0], mod[:, 1], mod[:, 2], mod[:, 3], mod[:, 4], mod[:, 5])
    ga = (2 * (ga >= 0) - 1) * jnp.maximum(jnp.abs(ga), 0.25)
    gb = (2 * (gb >= 0) - 1) * jnp.maximum(jnp.abs(gb), 0.25)
    h = _layernorm(x, axis=-1) * (1 + ca) + sa
    x = x + ga * _L0_attn_ref(h, L0_attn_Wq_w, L0_attn_Wq_b, L0_attn_Wk_w, L0_attn_Wk_b, L0_attn_Wv_w, L0_attn_Wv_b, L0_attn_Wo_w, L0_attn_Wo_b)
    h = _layernorm(x, axis=-1) * (1 + cb) + sb
    x = x + gb * _L0_ffn_ref(h, L0_ffn_cond, L0_ffn_mask, L0_ffn_W_shared, L0_ffn_W_expert, L0_ffn_W_gate, L0_ffn_bias)
    return x

_drawn_inputs = setup_inputs


def setup_inputs(seed=0):
    import zlib

    import numpy as np

    out = dict(_drawn_inputs(seed))
    spreads = {'L0_ffn_bias': (0.0, 0.31)}
    factors = {'L0_attn_Wq_w': 8.0,
     'L0_attn_Wq_b': 8.0,
     'L0_attn_Wk_w': 8.0,
     'L0_attn_Wk_b': 8.0,
     'L0_attn_Wv_w': 8.0,
     'L0_attn_Wv_b': 8.0,
     'L0_attn_Wo_w': 8.0,
     'L0_attn_Wo_b': 8.0,
     'L0_ffn_W_gate': 8.0}
    for name, (base, spread) in spreads.items():
        noise = np.random.default_rng([zlib.crc32(name.encode()), seed]).standard_normal(out[name].shape)
        drawn = base * np.exp(spread * noise) if base else spread * noise
        out[name] = jnp.asarray(drawn.astype(out[name].dtype))
    for name, factor in factors.items():
        out[name] = (out[name] * factor).astype(out[name].dtype)
    return out
```

```python
from contextlib import ExitStack

import concourse.bass as bass
from concourse import mybir
from concourse.alu_op_type import AluOpType as ALU

ACT = mybir.ActivationFunctionType
AX = mybir.AxisListType
F32 = mybir.dt.float32
BF16 = mybir.dt.bfloat16

P = 128
B, T, D = 4, 1024, 256
H, DH = 16, 16
NB = T // P
KT = D // P
CH = 512
NC = T // CH
HG = 4
NG = H // HG
E_GATE = 7
LN_EPS = 1e-5
GATE_FLOOR = 0.25
SCORE_SCALE = 1.0 / D ** 0.5
MASKED = -3.0e38

Q_PARTS = (0, 0, 1, 1, 0, 2)
K_PARTS = (0, 1, 0, 1, 2, 0)
ROWS = DH * len(Q_PARTS)
MROWS = 3

MOD_SA, MOD_CA, MOD_GA, MOD_SB, MOD_CB, MOD_GB = range(6)


def max_tiles():
    tiles = []
    for i in range(NB):
        for half in range(2):
            keys = min((i + 1) * P - half * CH, CH)
            if keys <= 0:
                continue
            heads = max(n for n in (1, 2, 4) if n * keys <= CH)
            for h in range(0, HG, heads):
                tiles.append((i, half, h, heads, half * CH, keys))
    return tiles


def units():
    out = []
    for c in range(NC):
        for j in range((c + 1) * CH // P):
            first = max(c * CH, j * P)
            out.append((c, j, first, (c + 1) * CH - first, j * P >= c * CH))
    return out


MAX_TILES = max_tiles()
UNITS = units()
NMT, NU = len(MAX_TILES), len(UNITS)
NEXP = 2 * NU
NDIAG = sum(u[4] for u in UNITS)
NP_BUF = 3
CHUNK_END = [sum(u[0] <= c for u in UNITS) for c in range(NC)]


def schedule():
    cost = [t[3] * t[5] for t in MAX_TILES]
    widths = [u[3] for u in UNITS]
    out, done, n = [], 0, 0
    for u in range(NU):
        share = sum(cost) * sum(widths[:u + 1]) / sum(widths[:NU - 2])
        while n < NMT and done < share:
            done += cost[n]
            n += 1
        out.append(n)
    return out


SCHEDULE = schedule()


def adaln_block(nc, x, wq_t, wk_t, wv_t, wo_t, ws_t, we_t, wgate, bq, bk, bv, bo, bf, c_t, wmod, out):
    with ExitStack() as ctx:
        def sb(name, shape, dt=F32):
            return ctx.enter_context(nc.sbuf_tensor(name, shape, dt))

        def pb(name, shape, dt=F32):
            return ctx.enter_context(nc.psum_tensor(name, shape, dt))

        def sem(name):
            return ctx.enter_context(nc.semaphore(name))

        counted = []

        def counted_sem(name):
            counted.append(sem(name))
            return counted[-1]

        def after(n):
            return n + 1

        wq = sb("wq", [P, KT, D])
        wk = sb("wk", [P, KT, D])
        wv = sb("wv", [P, KT, D])
        wo = sb("wo", [P, KT, D])
        wse = sb("wse", [P, KT, 2 * D])
        wg = sb("wg", [P, KT, E_GATE])
        wo_g = sb("wo_g", [P, KT, D])
        wse_g = sb("wse_g", [P, KT, 2 * D])
        bqk = sb("bqk", [P, 2, KT])
        bv_bc = sb("bv_bc", [P, D])
        bob_bc = sb("bob_bc", [P, 2, D])
        gate_bc = sb("gate_bc", [P, B, 2, D])
        gbias = sb("gbias", [P, 2, D])
        modc = sb("modc", [P, 6, KT, B])
        ct = sb("ct", [P, KT, B])
        ect = sb("ect", [P, KT, B])
        silu = sb("silu", [P, KT, B])
        grow = sb("grow", [B, 2 * D])
        sel = sb("sel", [B, B, P])
        ident = sb("ident", [P, P])
        ident_b = sb("ident_b", [P, P], BF16)
        mask_b = sb("mask_b", [P, P], BF16)
        nhalf = sb("nhalf", [P, NB])
        xs = sb("xs", [P, NB, D])
        xg = sb("xg", [P, NB, D])
        xn = sb("xn", [P, NB, D])
        ht = sb("ht", [P, KT, T])
        stats = sb("stats", [P, NB, 6])
        mv = sb("mv", [P, NB, 2])
        ve = sb("ve", [P, NB])
        rstd = sb("rstd", [P, NB])
        stage = sb("stage", [P, 2, CH])
        gsign, gabs = stage[0:B, 0, :], stage[0:B, 1, :]
        rest = sb("rest", [P, 2, CH])
        parts = sb("parts", [P, 2, 3, KT, T], BF16)
        wm = parts[:, 0, :, :, :].rearrange("p r k n -> p (r k n)").bitcast(F32).rearrange("p (k n) -> p k n", k=KT)
        v = sb("v", [P, NB, H, 2 * DH])
        qs = [sb(f"qs{i}", [P, HG, T], BF16) for i in range(2)]
        ks = [sb(f"ks{i}", [P, HG, T], BF16) for i in range(2)]
        mpart = sb("mpart", [P, HG, NB, 2])
        mx = sb("mx", [P, HG * NB])
        mrest = sb("mrest", [P, HG * NB])
        m3 = sb("m3", [P, MROWS, HG * NB], BF16)
        mrow = sb("mrow", [MROWS * HG * NB, P], BF16)
        probs = [sb(f"probs{i}", [P, HG, CH]) for i in range(NP_BUF)]
        ot = sb("ot", [P, NG, T])
        rec = sb("rec", [P, 2, H])
        on = sb("on", [P, 2, H, DH])
        ont = sb("ont", [P, 2, KT, P])
        x1 = sb("x1", [P, NB, D])
        logit = sb("logit", [P, NB, 8])
        lmax = sb("lmax", [P, NB])
        lexp = sb("lexp", [P, NB, 8])
        lsum = sb("lsum", [P, NB])
        score = sb("score", [P, NB, 8])
        top8 = sb("top8", [P, NB, 8])
        tsum = sb("tsum", [P, NB])
        wtop = sb("wtop", [P, NB, 2])
        wsum = sb("wsum", [P, NB])
        y = sb("y", [P, 2, D])

        ps_t = [pb(f"ps_t{i}", [P, 2, CH]) for i in range(2)]
        work = [ps_t[i // 2][:, i % 2, :] for i in range(4)]
        ps_m = [pb(f"ps_m{i}", [P, CH]) for i in range(2)]
        ps_o = pb("ps_o", [P, CH])
        ps_x = pb("ps_x", [P, CH])
        ps_mt = ps_x[:, 0:P // 2].bitcast(BF16)

        scratch = nc.dram_tensor("parts_scratch", [B, 2, 3, D, T], BF16, kind="Internal").ap()

        w_loaded = sem("w_loaded")
        x_loaded = counted_sem("x_loaded")
        pool_const = sem("pool_const")
        dve_const = sem("dve_const")
        c_exp = sem("c_exp")
        silu_step = sem("silu_step")
        mod_mm = sem("mod_mm")
        mod_step = sem("mod_step")
        gate_ready = sem("gate_ready")
        bc_mm = sem("bc_mm")
        bc_evac = sem("bc_evac")
        gbias_ready = counted_sem("gbias_ready")
        w_scaled = counted_sem("w_scaled")
        ln_stats = counted_sem("ln_stats")
        ln_mv = counted_sem("ln_mv")
        ln_rstd = counted_sem("ln_rstd")
        xn_ready = counted_sem("xn_ready")
        h_tr = counted_sem("h_tr")
        h_ready = counted_sem("h_ready")
        xg_ready = counted_sem("xg_ready")
        qk_mm = counted_sem("qk_mm")
        qk_evac = counted_sem("qk_evac")
        p1_ready = counted_sem("p1_ready")
        r_ready = counted_sem("r_ready")
        p2_ready = counted_sem("p2_ready")
        p3_ready = counted_sem("p3_ready")
        parts_stored = [counted_sem(f"parts_stored{i}") for i in range(KT)]
        stack_loaded = [counted_sem(f"stack_loaded{i}") for i in range(2)]
        v_mm = counted_sem("v_mm")
        v_ready = counted_sem("v_ready")
        s_mm = counted_sem("s_mm")
        s_red = counted_sem("s_red")
        m_step = counted_sem("m_step")
        m3_ready = counted_sem("m3_ready")
        m_tr = counted_sem("m_tr")
        mrow_ready = counted_sem("mrow_ready")
        mrow_loaded = [counted_sem(f"mrow_loaded{i}") for i in range(2)]
        st_mm = counted_sem("st_mm")
        exp_done = counted_sem("exp_done")
        diag_done = counted_sem("diag_done")
        pv_done = counted_sem("pv_done")
        po_evac = counted_sem("po_evac")
        o_tr = counted_sem("o_tr")
        rec_ready = counted_sem("rec_ready")
        on_ready = counted_sem("on_ready")
        on_tr = counted_sem("on_tr")
        ont_ready = counted_sem("ont_ready")
        wo_mm = counted_sem("wo_mm")
        x1_ready = counted_sem("x1_ready")
        x1b_ready = counted_sem("x1b_ready")
        gate_mm = counted_sem("gate_mm")
        g_step = counted_sem("g_step")
        g_exp = counted_sem("g_exp")
        ffn_mm = counted_sem("ffn_mm")
        y_ready = counted_sem("y_ready")
        out_ready = counted_sem("out_ready")
        out_stored = counted_sem("out_stored")

        N_WLOADS = 14
        G_STEPS = 6 + NB + 4

        xv = x.rearrange("b (n p) d -> b p n d", p=P)
        ov = out.rearrange("b (n p) d -> b p n d", p=P)

        def apart(engine):
            engine.nop(nofuse=True)

        block = ctx.enter_context(nc.Block())

        @block.sync
        def _(sp):
            def load_x(b):
                sp.dma_start(xs[:, :, :], xv[bass.ds(b, 1)].rearrange("o p n d -> (o p) n d")).then_inc(x_loaded, 16)

            def store_parts(b, mt):
                for which in range(2):
                    sp.wait_ge(p3_ready, after(8 * b + 4 * mt + 2 * which + 2))
                    for part in range(3):
                        sp.dma_start(scratch[bass.ds(b, 1), which, part, mt * P:(mt + 1) * P, :]
                                     .rearrange("o p n -> (o p) n"),
                                     parts[:, which, part, mt, :]).then_inc(parts_stored[mt], 16)

            def load_stacks(b, t):
                sp.wait_ge(parts_stored[t // 2], after(96 * b + 96))
                apart(sp)
                sp.wait_ge(st_mm, after(NEXP * (NG * b + max(t - 1, 0))))
                f0 = t * HG * DH
                for which, dst, order in ((0, qs, Q_PARTS), (1, ks, K_PARTS)):
                    for r, part in enumerate(order):
                        src = scratch[bass.ds(b, 1), which, part, f0:f0 + HG * DH, :]
                        sp.dma_start(dst[t % 2][r * DH:(r + 1) * DH, :, :],
                                     src.rearrange("o (h d) n -> (o d) h n", d=DH)
                                     ).then_inc(stack_loaded[t % 2], 16)

            def load_mrows(b, t):
                sp.wait_ge(mrow_ready, after(4 * b + t + 1))
                n = HG * NB
                for r in range(MROWS):
                    sp.dma_start(qs[t % 2][ROWS + r:ROWS + r + 1, :, :].rearrange("o h (i q) -> o (h i) q", q=P),
                                 mrow[r * n:(r + 1) * n, :]).then_inc(mrow_loaded[t % 2], 16)

            for s in counted:
                sp.sem_inc(s, 1)
            sp.dma_start(xs[:, :, :], xv[0]).then_inc(x_loaded, 16)
            for dst, src in ((wq, wq_t), (wk, wk_t), (wv, wv_t), (wo, wo_t)):
                sp.dma_start(dst[:, :, :], src.rearrange("(k p) n -> p k n", p=P)).then_inc(w_loaded, 16)
            sp.dma_start(wse[:, :, 0:D], ws_t.rearrange("(k p) n -> p k n", p=P)).then_inc(w_loaded, 16)
            sp.dma_start(wse[:, :, D:2 * D], we_t.rearrange("(k p) n -> p k n", p=P)).then_inc(w_loaded, 16)
            sp.dma_start(wg[:, :, :], wgate.rearrange("(k p) n -> p k n", p=P)).then_inc(w_loaded, 16)
            sp.dma_start(bqk[:, 0, :], bq).then_inc(w_loaded, 16)
            sp.dma_start(bqk[:, 1, :], bk).then_inc(w_loaded, 16)
            for dst, src in ((bv_bc[:, :], bv), (bob_bc[:, 0, :], bo), (bob_bc[:, 1, :], bf)):
                sp.dma_start(dst, src.to_broadcast([P, D])).then_inc(w_loaded, 16)
            sp.dma_start(ct[:, :, :], c_t.rearrange("(k p) n -> p k n", p=P)).then_inc(w_loaded, 16)
            sp.dma_start(wm[:, :, :], wmod.rearrange("(k p) n -> p k n", p=P)).then_inc(w_loaded, 16)
            def batch(b, more):
                store_parts(b, 0)
                load_stacks(b, 0)
                store_parts(b, 1)
                load_stacks(b, 1)
                load_mrows(b, 0)
                if more:
                    next_batch = sp.snap(b + 1)
                    sp.wait_ge(xn_ready, after(2 * NB * b + NB))
                    sp.wait_ge(xg_ready, after(NB * b + NB))
                    apart(sp)
                    load_x(next_batch)
                load_mrows(b, 1)
                load_stacks(b, 2)
                load_mrows(b, 2)
                load_stacks(b, 3)
                load_mrows(b, 3)
                for half in range(2):
                    n0 = half * NB // 2
                    sp.wait_ge(out_ready, after(NB * b + n0 + NB // 2))
                    sp.dma_start(ov[bass.ds(b, 1), :, n0:n0 + NB // 2, :].rearrange("o p n d -> (o p) n d"),
                                 x1[:, n0:n0 + NB // 2, :]).then_inc(out_stored, 16)

            with sp.Fori(0, B - 1) as b:
                batch(b, True)
            batch(B - 1, False)
            sp.wait_ge(out_stored, after(2 * 16 * B))
            for mt in range(KT):
                sp.wait_ge(parts_stored[mt], after(96 * B))

        @block.gpsimd
        def _(pool):
            def consts():
                pool.memset(ident[:, :], 0.0).then_inc(pool_const, 1)
                pool.memset(ident_b[:, :], 0.0).then_inc(pool_const, 1)
                pool.memset(mask_b[:, :], 0.0).then_inc(pool_const, 1)
                pool.memset(sel[:, :, :], 0.0).then_inc(pool_const, 1)
                pool.memset(nhalf[:, :], -0.5).then_inc(pool_const, 1)
                pool.wait_ge(pool_const, 5)
                for m in (ident, ident_b):
                    pool.affine_select(out=m[:, :], in_=m[:, :], compare_op=ALU.not_equal, fill=1.0, base=0,
                                       pattern=[[-1, P]], channel_multiplier=1).then_inc(pool_const, 1)
                pool.affine_select(out=mask_b[:, :], in_=mask_b[:, :], compare_op=ALU.is_ge, fill=MASKED,
                                   base=0, pattern=[[-1, P]], channel_multiplier=1).then_inc(pool_const, 1)
                pool.affine_select(out=sel[:, :, :], in_=sel[:, :, :], compare_op=ALU.not_equal, fill=1.0,
                                   base=0, pattern=[[-1, B], [0, P]], channel_multiplier=1).then_inc(pool_const, 1)

            def scale_weights(b):
                pool.wait_ge(wo_mm, after(NB * b))
                pool.wait_ge(ffn_mm, after(NB * b))
                ga = gate_bc[:, bass.ds(b, 1), 0, :]
                gb = gate_bc[:, bass.ds(b, 1), 1, :]
                for e, g in enumerate((ga, gb)):
                    pool.tensor_tensor(gbias[:, e:e + 1, :], bob_bc[:, e:e + 1, :], g, ALU.mult).then_inc(gbias_ready, 1)
                for k in range(KT):
                    pool.tensor_tensor(wo_g[:, k:k + 1, :], wo[:, k:k + 1, :], ga, ALU.mult).then_inc(w_scaled, 1)
                    for e in range(2):
                        pool.tensor_tensor(wse_g[:, k:k + 1, e * D:(e + 1) * D], wse[:, k:k + 1, e * D:(e + 1) * D],
                                           gb, ALU.mult).then_inc(w_scaled, 1)

            def rstd_of(n):
                pool.wait_ge(ln_mv, after(NB * n + NB))
                pool.wait_ge(xn_ready, after(NB * n))
                apart(pool)
                pool.tensor_scalar(ve[:, :], mv[:, :, 1], LN_EPS, None, ALU.add).then_inc(ln_rstd, 1)
                pool.wait_ge(ln_rstd, after(2 * n + 1))
                pool.tensor_tensor(rstd[:, :], ve[:, :], nhalf[:, :], ALU.pow).then_inc(ln_rstd, 1)

            def add_bias(b, dst, src, which, ready):
                pool.wait_ge(gbias_ready, after(2 * b + 2))
                for i in range(NB):
                    pool.tensor_tensor(dst[:, i, :], src[:, i, :], gbias[:, which, :], ALU.add).then_inc(ready, 1)

            def rest_of(b, n):
                mt, which, c = n // 4, n // 2 % 2, n % 2
                pool.wait_ge(p1_ready, after(8 * b + n + 1))
                pool.wait_ge(p3_ready, after(8 * b + max(n - 1, 0)))
                pool.tensor_tensor(rest[:, n % 2, :], stage[:, n % 2, :],
                                   parts[:, which, 0, mt, c * CH:(c + 1) * CH], ALU.subtract).then_inc(r_ready, 1)

            def third(b, n):
                mt, which, c = n // 4, n // 2 % 2, n % 2
                pool.wait_ge(p2_ready, after(8 * b + n + 1))
                pool.tensor_tensor(parts[:, which, 2, mt, c * CH:(c + 1) * CH], rest[:, n % 2, :],
                                   parts[:, which, 1, mt, c * CH:(c + 1) * CH], ALU.subtract).then_inc(p3_ready, 1)

            def diagonals(b, t):
                d = 0
                for u, (c, j, first, width, diagonal) in enumerate(UNITS):
                    if not diagonal:
                        continue
                    pool.wait_ge(exp_done, after(NEXP * (4 * b + t) + 2 * u + 2))
                    pr = probs[u % NP_BUF][:, :, 0:P]
                    apart(pool)
                    pool.affine_select(out=pr, in_=pr, compare_op=ALU.is_ge, fill=0.0, base=0,
                                       pattern=[[0, HG], [1, P]], channel_multiplier=-1).then_inc(diag_done, 1)
                    d += 1

            consts()
            pool.wait_ge(bc_evac, B)
            pool.wait_ge(w_loaded, 16 * N_WLOADS)
            with pool.Fori(0, B) as b:
                rstd_of(2 * b)
                for n in range(9):
                    if n < 8:
                        rest_of(b, n)
                    if n >= 1:
                        third(b, n - 1)
                scale_weights(b)
                pool.wait_ge(x_loaded, after(16 * b + 16))
                pool.wait_ge(x1_ready, after(NB * b))
                add_bias(b, xg, xs, 0, xg_ready)
                for t in range(NG):
                    diagonals(b, t)
                rstd_of(2 * b + 1)
                pool.wait_ge(xn_ready, after(NB * (2 * b + 1) + NB))
                add_bias(b, x1, x1, 1, x1b_ready)

        @block.scalar
        def _(act):
            def modulate(b, second):
                s, c = (MOD_SB, MOD_CB) if second else (MOD_SA, MOD_CA)
                for i in range(4):
                    k, ch = i // 2, i % 2
                    act.wait_ge(h_tr, after(4 * (2 * b + second) + i + 1))
                    apart(act)
                    act.activation(ht[:, k, ch * CH:(ch + 1) * CH], work[i], ACT.Identity,
                                   bias=modc[:, s, k, bass.ds(b, 1)], scale=modc[:, c, k, bass.ds(b, 1)]
                                   ).then_inc(h_ready, 1)

            def qk_evacuate(b):
                for n in range(8):
                    mt, which = n // 4, n // 2 % 2
                    act.wait_ge(qk_mm, after(8 * b + n + 1))
                    act.wait_ge(r_ready, after(8 * b + max(n - 1, 0)))
                    act.activation(stage[:, n % 2, :], work[n % 4], ACT.Identity,
                                   bias=bqk[:, which, mt:mt + 1]).then_inc(qk_evac, 1)

            def exps(b, t):
                for u, (c, j, first, width, diagonal) in enumerate(UNITS):
                    for pr in range(2):
                        act.wait_ge(st_mm, after(NEXP * (4 * b + t) + 2 * u + pr + 1))
                        if pr == 0:
                            if t == 0 and u < NP_BUF:
                                act.wait_ge(pv_done, after(NG * NU * b))
                            else:
                                act.wait_ge(pv_done, after(NG * NU * b + NU * t + u - NP_BUF + 1))
                        act.activation(probs[u % NP_BUF][:, 2 * pr:2 * pr + 2, 0:width], ps_t[pr][:, :, 0:width],
                                       ACT.Exp, scale=SCORE_SCALE).then_inc(exp_done, 1)

            def on_evacuate(b):
                for i in range(NB):
                    act.wait_ge(on_tr, after(NB * b + i + 1))
                    act.wait_ge(wo_mm, after(NB * b + max(i - 1, 0)))
                    act.activation(ont[:, i % 2, :, :], ps_m[i % 2][:, 0:D].rearrange("p (k n) -> p k n", k=KT),
                                   ACT.Copy).then_inc(ont_ready, 1)

            act.wait_ge(w_loaded, 16 * N_WLOADS)
            act.activation(ect[:, :, :], ct[:, :, :], ACT.Exp, scale=-1.0).then_inc(c_exp, 1)
            act.wait_ge(mod_step, 3)
            with act.Fori(0, B) as b:
                modulate(b, 0)
                qk_evacuate(b)
                for t in range(NG):
                    exps(b, t)
                on_evacuate(b)
                modulate(b, 1)
                act.wait_ge(g_step, after(G_STEPS * b + 3))
                act.activation(lexp[:, :, :], lexp[:, :, :], ACT.Exp).then_inc(g_exp, 1)

        @block.vector
        def _(dve):
            def spread(a, n):
                return a[:, :].rearrange("p (i o) -> p i o", o=1).to_broadcast([P, NB, n])

            def statistics(n, src, i):
                dve.bn_stats(stats[:, i, :], src[:, i, :]).then_inc(ln_stats, 1)

            def aggregate(n):
                for i in range(NB):
                    dve.wait_ge(ln_stats, after(NB * n + i + 1))
                    apart(dve)
                    dve.bn_aggr(mv[:, i, :], stats[:, i, :]).then_inc(ln_mv, 1)

            def normalise(n, src):
                dve.wait_ge(ln_rstd, after(2 * n + 2))
                dve.wait_ge(h_tr, after(4 * n))
                for i in range(NB):
                    dve.tensor_scalar(xn[:, i, :], src[:, i, :], mv[:, i, 0:1], rstd[:, i:i + 1],
                                      ALU.subtract, ALU.mult).then_inc(xn_ready, 1)

            def split(b):
                for n in range(9):
                    if n < 8:
                        mt, which, c = n // 4, n // 2 % 2, n % 2
                        if n % 4 == 0:
                            dve.wait_ge(parts_stored[mt], after(96 * b))
                        dve.wait_ge(qk_evac, after(8 * b + n + 1))
                        dve.tensor_copy(parts[:, which, 0, mt, c * CH:(c + 1) * CH],
                                        stage[:, n % 2, :]).then_inc(p1_ready, 1)
                    if n >= 1:
                        m = n - 1
                        mt, which, c = m // 4, m // 2 % 2, m % 2
                        dve.wait_ge(r_ready, after(8 * b + m + 1))
                        dve.tensor_copy(parts[:, which, 1, mt, c * CH:(c + 1) * CH],
                                        rest[:, m % 2, :]).then_inc(p2_ready, 1)

            def values(b):
                dve.wait_ge(pv_done, after(NG * NU * b))
                for n in range(NB // 2):
                    dve.wait_ge(v_mm, after(NB // 2 * b + n + 1))
                    for i in range(2):
                        ins = dve.tensor_tensor(v[:, 2 * n + i, :, 0:DH],
                                                work[n][:, i * D:(i + 1) * D].rearrange("p (h d) -> p h d", d=DH),
                                                bv_bc[:, :].rearrange("p (h d) -> p h d", d=DH), ALU.add)
                        ins.then_inc(v_ready, 1)

            def maxima(b, t, k):
                i, half, h0, heads, key0, keys = MAX_TILES[k]
                dve.wait_ge(s_mm, after(NMT * (4 * b + t) + k + 1))
                dve.tensor_reduce(mpart[:, h0:h0 + heads, i, half],
                                  ps_m[k % 2][:, 0:heads * keys].rearrange("p (h n) -> p h n", h=heads),
                                  AX.X, ALU.max).then_inc(s_red, 1)

            def split_maxima(b, t):
                base = 4 * (4 * b + t)
                dve.wait_ge(s_red, after(NMT * (4 * b + t) + NMT))
                dve.tensor_reduce(mx[:, :], mpart[:, :, :, :].rearrange("p h i a -> p (h i) a"),
                                  AX.X, ALU.max).then_inc(m_step, 1)
                dve.wait_ge(m_step, after(base + 1))
                dve.wait_ge(m_tr, after(4 * b + t))
                dve.tensor_scalar(m3[:, 0, :], mx[:, :], -1.0, None, ALU.mult).then_inc(m_step, 1)
                dve.wait_ge(m_step, after(base + 2))
                dve.scalar_tensor_tensor(out=mrest[:, :], in0=mx[:, :], scalar=-1.0, in1=m3[:, 0, :],
                                         op0=ALU.mult, op1=ALU.subtract).then_inc(m_step, 1)
                dve.wait_ge(m_step, after(base + 3))
                dve.tensor_copy(m3[:, 1, :], mrest[:, :]).then_inc(m_step, 1)
                dve.wait_ge(m_step, after(base + 4))
                dve.tensor_tensor(m3[:, 2, :], mrest[:, :], m3[:, 1, :], ALU.subtract).then_inc(m3_ready, 1)

            def maxima_rows(b, t):
                dve.wait_ge(m_tr, after(4 * b + t + 1))
                if t == 0:
                    dve.wait_ge(mrow_loaded[1], after(96 * b))
                else:
                    dve.wait_ge(mrow_loaded[(t - 1) % 2], after(96 * b + 48 * ((t - 1) // 2 + 1)))
                dve.tensor_copy(mrow[:, :], ps_mt[0:MROWS * HG * NB, :]).then_inc(mrow_ready, 1)

            def out_evacuate(b, t, c):
                dve.wait_ge(pv_done, after(NU * (4 * b + t) + CHUNK_END[c]))
                if t == 0:
                    dve.wait_ge(o_tr, after(NB * b))
                dve.tensor_copy(ot[:, t, c * CH:(c + 1) * CH], ps_o[:, :]).then_inc(po_evac, 1)

            def attention(b, t):
                k = 0
                for u in range(NU):
                    while t + 1 < NG and k < NMT and k < SCHEDULE[u]:
                        maxima(b, t + 1, k)
                        k += 1
                    if u == CHUNK_END[0]:
                        out_evacuate(b, t, 0)
                if t + 1 < NG:
                    split_maxima(b, t + 1)
                    maxima_rows(b, t + 1)
                out_evacuate(b, t, 1)

            def project_out(b):
                for i in range(NB + 2):
                    if i < NB:
                        dve.wait_ge(o_tr, after(NB * b + i + 1))
                        o3 = work[i % 4].rearrange("p (h r) -> p h r", r=2 * DH)
                        dve.reciprocal(rec[:, i % 2, :], o3[:, :, DH]).then_inc(rec_ready, 1)
                        dve.wait_ge(rec_ready, after(NB * b + i + 1))
                        dve.wait_ge(on_tr, after(NB * b + max(i - 1, 0)))
                        dve.tensor_tensor(on[:, i % 2, :, :], o3[:, :, 0:DH],
                                          rec[:, i % 2, :].rearrange("p (h o) -> p h o", o=1).to_broadcast([P, H, DH]),
                                          ALU.mult).then_inc(on_ready, 1)
                    if i >= 2:
                        m = i - 2
                        dve.wait_ge(wo_mm, after(NB * b + m + 1))
                        if m == 0:
                            dve.wait_ge(xg_ready, after(NB * b + NB))
                            dve.wait_ge(out_stored, after(32 * b))
                        dve.tensor_tensor(x1[:, m, :], [ps_x, ps_o][m % 2][:, 0:D], xg[:, m, :],
                                          ALU.add).then_inc(x1_ready, 1)
                        dve.wait_ge(x1_ready, after(NB * b + m + 1))
                        statistics(2 * b + 1, x1, m)

            def gate(b):
                step = [0]

                def link(ins):
                    step[0] += 1
                    ins.then_inc(g_step, 1)
                    dve.wait_ge(g_step, after(G_STEPS * b + step[0]))

                dve.wait_ge(gate_mm, after(b + 1))
                link(dve.tensor_copy(logit[:, :, 0:E_GATE],
                                     ps_x[:, 0:8 * NB].rearrange("p (i e) -> p i e", e=8)[:, :, 0:E_GATE]))
                link(dve.tensor_reduce(lmax[:, :], logit[:, :, :], AX.X, ALU.max))
                link(dve.tensor_tensor(lexp[:, :, :], logit[:, :, :], spread(lmax, 8), ALU.subtract))
                dve.wait_ge(g_exp, after(b + 1))
                link(dve.tensor_reduce(lsum[:, :], lexp[:, :, :], AX.X, ALU.add))
                link(dve.reciprocal(lsum[:, :], lsum[:, :]))
                link(dve.tensor_tensor(score[:, :, :], lexp[:, :, :], spread(lsum, 8), ALU.mult))
                for i in range(NB):
                    apart(dve)
                    link(dve.max(top8[:, i, :], score[:, i, :]))
                link(dve.tensor_reduce(tsum[:, :], top8[:, :, 0:2], AX.X, ALU.add))
                link(dve.reciprocal(tsum[:, :], tsum[:, :]))
                link(dve.tensor_tensor(wtop[:, :, :], top8[:, :, 0:2], spread(tsum, 2), ALU.mult))
                link(dve.tensor_reduce(wsum[:, :], wtop[:, :, :], AX.X, ALU.add))

            def finish(b):
                dve.wait_ge(x1b_ready, after(NB * b + NB))
                for i in range(NB):
                    dve.wait_ge(ffn_mm, after(NB * b + i + 1))
                    dve.scalar_tensor_tensor(out=y[:, i % 2, :], in0=work[i % 4][:, D:2 * D],
                                             scalar=wsum[:, i:i + 1], in1=x1[:, i, :],
                                             op0=ALU.mult, op1=ALU.add).then_inc(y_ready, 1)
                    dve.wait_ge(y_ready, after(NB * b + i + 1))
                    dve.tensor_tensor(x1[:, i, :], work[i % 4][:, 0:D], y[:, i % 2, :], ALU.add).then_inc(out_ready, 1)

            def modulation():
                dve.wait_ge(c_exp, 1)
                dve.tensor_scalar(ect[:, :, :], ect[:, :, :], 1.0, None, ALU.add).then_inc(silu_step, 1)
                dve.wait_ge(silu_step, 1)
                dve.reciprocal(ect[:, :, :], ect[:, :, :]).then_inc(silu_step, 1)
                dve.wait_ge(silu_step, 2)
                dve.tensor_tensor(silu[:, :, :], ct[:, :, :], ect[:, :, :], ALU.mult).then_inc(silu_step, 1)
                dve.wait_ge(mod_mm, 2)
                dve.tensor_copy(modc[:, :, :, :].rearrange("p m k b -> p (m k b)"),
                                ps_x[:, 0:6 * KT * B]).then_inc(mod_step, 1)
                dve.wait_ge(mod_step, 1)
                for m in (MOD_CA, MOD_CB):
                    dve.tensor_scalar(modc[:, m, :, :], modc[:, m, :, :], 1.0, None, ALU.add).then_inc(mod_step, 1)
                dve.tensor_copy(grow[:, :], ps_o[0:B, :]).then_inc(mod_step, 1)
                dve.wait_ge(mod_step, 4)
                dve.tensor_scalar(gsign, grow[:, :], 0.0, 2.0, ALU.is_ge, ALU.mult).then_inc(mod_step, 1)
                dve.scalar_tensor_tensor(out=gabs, in0=grow[:, :], scalar=-1.0, in1=grow[:, :],
                                         op0=ALU.mult, op1=ALU.max).then_inc(mod_step, 1)
                dve.wait_ge(mod_step, 6)
                dve.tensor_scalar(gabs, gabs, GATE_FLOOR, None, ALU.max).then_inc(mod_step, 1)
                dve.wait_ge(mod_step, 7)
                dve.scalar_tensor_tensor(out=grow[:, :], in0=gsign, scalar=-1.0, in1=gabs,
                                         op0=ALU.add, op1=ALU.mult).then_inc(gate_ready, 1)
                for b in range(B):
                    dve.wait_ge(bc_mm, b + 1)
                    dve.tensor_copy(gate_bc[:, b, :, :].rearrange("p a d -> p (a d)"), work[b]).then_inc(bc_evac, 1)

            dve.memset(v[:, :, :, DH:2 * DH], 1.0).then_inc(dve_const, 1)
            dve.memset(mpart[:, :, :, :], MASKED).then_inc(dve_const, 1)
            dve.memset(logit[:, :, :], MASKED).then_inc(dve_const, 1)
            for i in range(2):
                dve.memset(ks[i][ROWS:ROWS + MROWS, :, :], 1.0).then_inc(dve_const, 1)
            dve.wait_ge(dve_const, 5)
            modulation()
            with dve.Fori(0, B) as b:
                dve.wait_ge(x_loaded, after(16 * b + 16))
                for i in range(NB):
                    statistics(2 * b, xs, i)
                aggregate(2 * b)
                normalise(2 * b, xs)
                split(b)
                values(b)
                for k in range(NMT):
                    maxima(b, 0, k)
                split_maxima(b, 0)
                maxima_rows(b, 0)
                for t in range(NG):
                    attention(b, t)
                project_out(b)
                aggregate(2 * b + 1)
                normalise(2 * b + 1, x1)
                gate(b)
                finish(b)

        @block.tensor
        def _(pe):
            def transpose_h(n):
                for i in range(4):
                    k, ch = i // 2, i % 2
                    if k == 0:
                        pe.wait_ge(xn_ready, after(NB * n + 4 * ch + 4))
                    for q in range(4):
                        blk = 4 * ch + q
                        mm = pe.transpose(work[i][:, q * P:(q + 1) * P], xn[:, blk, k * P:(k + 1) * P], ident[:, :])
                    mm.then_inc(h_tr, 1)

            def project_qk(b):
                pe.wait_ge(h_ready, after(4 * (2 * b) + 4))
                for n in range(8):
                    mt, which, c = n // 4, n // 2 % 2, n % 2
                    if n >= 4:
                        pe.wait_ge(qk_evac, after(8 * b + n - 3))
                    for k in range(KT):
                        mm = pe.matmul(work[n % 4], (wq, wk)[which][:, k, mt * P:(mt + 1) * P],
                                       ht[:, k, c * CH:(c + 1) * CH], start=(k == 0), stop=(k == KT - 1))
                    mm.then_inc(qk_mm, 1)

            def project_v(b):
                for n in range(NB // 2):
                    pe.wait_ge(qk_evac, after(8 * b + 5 + n))
                    for i in range(2):
                        blk = 2 * n + i
                        for k in range(KT):
                            mm = pe.matmul(work[n][:, i * D:(i + 1) * D], ht[:, k, blk * P:(blk + 1) * P],
                                           wv[:, k, :], start=(k == 0), stop=(k == KT - 1))
                    mm.then_inc(v_mm, 1)

            def scores(b, t, k):
                i, half, h0, heads, key0, keys = MAX_TILES[k]
                if k == 0:
                    pe.wait_ge(stack_loaded[t % 2], after(192 * (2 * b + t // 2) + 192))
                pe.wait_ge(s_red, after(NMT * (4 * b + t) + max(k - 1, 0)))
                for h in range(heads):
                    hh = h0 + h
                    o = ps_m[k % 2][:, h * keys:(h + 1) * keys]
                    diagonal = key0 + keys == (i + 1) * P
                    mm = pe.matmul(o, qs[t % 2][0:ROWS, hh, i * P:(i + 1) * P], ks[t % 2][0:ROWS, hh, key0:key0 + keys],
                                   start=True, stop=not diagonal)
                    if diagonal:
                        mm = pe.matmul(o[:, keys - P:keys], ident_b[:, :], mask_b[:, :], start=False, stop=True)
                mm.then_inc(s_mm, 1)

            def transpose_maxima(b, t):
                pe.wait_ge(m3_ready, after(4 * b + t + 1))
                pe.transpose(ps_mt[0:MROWS * HG * NB, :], m3[:, :, :].rearrange("p r n -> p (r n)"),
                             ident_b[:, :]).then_inc(m_tr, 1)

            def scores_t(b, t, u):
                c, j, first, width, diagonal = UNITS[u]
                if u == 0:
                    pe.wait_ge(mrow_loaded[t % 2], after(48 * (2 * b + t // 2) + 48))
                for pr in range(2):
                    e = NEXP * t + 2 * u + pr
                    pe.wait_ge(exp_done, after(NEXP * NG * b + max(e - 1, 0)))
                    for h in range(2):
                        hh = 2 * pr + h
                        mm = pe.matmul(ps_t[pr][:, h, 0:width], ks[t % 2][0:ROWS + MROWS, hh, j * P:(j + 1) * P],
                                       qs[t % 2][0:ROWS + MROWS, hh, first:first + width], start=True, stop=True)
                    mm.then_inc(st_mm, 1)

            def weigh_values(b, t, u):
                c, j, first, width, diagonal = UNITS[u]
                last = u + 1 == NU or UNITS[u + 1][0] != c
                pe.wait_ge(exp_done, after(NEXP * (4 * b + t) + 2 * u + 2))
                if diagonal:
                    pe.wait_ge(diag_done, after(NDIAG * (4 * b + t) + sum(x[4] for x in UNITS[:u + 1])))
                if j == 0:
                    pe.wait_ge(po_evac, after(NC * (4 * b + t) + c))
                for hh in range(HG):
                    mm = pe.matmul(ps_o[32 * hh:32 * hh + 32, CH - width:CH], v[:, j, HG * t + hh, :],
                                   probs[u % NP_BUF][:, hh, 0:width], start=(j == 0), stop=last)
                mm.then_inc(pv_done, 1)

            def attention(b, t):
                k = 0
                for u in range(NU):
                    scores_t(b, t, u)
                    while t + 1 < NG and k < SCHEDULE[u]:
                        scores(b, t + 1, k)
                        k += 1
                    if u >= 1:
                        weigh_values(b, t, u - 1)
                if t + 1 < NG:
                    transpose_maxima(b, t + 1)
                weigh_values(b, t, NU - 1)

            def project_out(b):
                pe.wait_ge(po_evac, after(NC * NG * b + NC * NG))
                pe.wait_ge(w_scaled, after(6 * b + 6))
                for i in range(NB + 2):
                    if i < NB:
                        if i >= 4:
                            pe.wait_ge(on_ready, after(NB * b + i - 3))
                        for t in range(NG):
                            mm = pe.transpose(work[i % 4][:, t * P:(t + 1) * P], ot[:, t, i * P:(i + 1) * P], ident[:, :])
                        mm.then_inc(o_tr, 1)
                    if 1 <= i <= NB:
                        m = i - 1
                        pe.wait_ge(on_ready, after(NB * b + m + 1))
                        pe.wait_ge(ont_ready, after(NB * b + max(m - 1, 0)))
                        for k in range(KT):
                            mm = pe.transpose(ps_m[m % 2][:, k * P:(k + 1) * P],
                                              on[:, m % 2, 8 * k:8 * k + 8, :].rearrange("p h d -> p (h d)"), ident[:, :])
                        mm.then_inc(on_tr, 1)
                    if i >= 2:
                        m = i - 2
                        pe.wait_ge(ont_ready, after(NB * b + m + 1))
                        pe.wait_ge(x1_ready, after(NB * b + max(m - 1, 0)))
                        for k in range(KT):
                            mm = pe.matmul([ps_x, ps_o][m % 2][:, 0:D], ont[:, m % 2, k, :], wo_g[:, k, :],
                                           start=(k == 0), stop=(k == KT - 1))
                        mm.then_inc(wo_mm, 1)

            def gate_logits(b):
                pe.wait_ge(h_ready, after(4 * (2 * b + 1) + 4))
                pe.wait_ge(x1_ready, after(NB * b + NB))
                for i in range(NB):
                    for k in range(KT):
                        mm = pe.matmul(ps_x[:, 8 * i:8 * i + E_GATE], ht[:, k, i * P:(i + 1) * P], wg[:, k, :],
                                       start=(k == 0), stop=(k == KT - 1))
                mm.then_inc(gate_mm, 1)

            def ffn(b):
                for i in range(NB):
                    if i >= 4:
                        pe.wait_ge(out_ready, after(NB * b + i - 3))
                    for k in range(KT):
                        mm = pe.matmul(work[i % 4], ht[:, k, i * P:(i + 1) * P], wse_g[:, k, :],
                                       start=(k == 0), stop=(k == KT - 1))
                    mm.then_inc(ffn_mm, 1)

            pe.wait_ge(w_loaded, 16 * N_WLOADS)
            pe.wait_ge(silu_step, 3)
            for m in range(6 * KT):
                for k in range(KT):
                    mm = pe.matmul(ps_x[:, m * B:(m + 1) * B], wm[:, k, m * P:(m + 1) * P], silu[:, k, :],
                                   start=(k == 0), stop=(k == KT - 1))
            mm.then_inc(mod_mm, 1)
            for e, m in enumerate((MOD_GA, MOD_GB)):
                for k in range(KT):
                    mm = pe.matmul(ps_o[0:B, e * D:(e + 1) * D], silu[:, k, :], wm[:, k, m * D:(m + 1) * D],
                                   start=(k == 0), stop=(k == KT - 1))
            mm.then_inc(mod_mm, 1)
            pe.wait_ge(gate_ready, 1)
            pe.wait_ge(pool_const, 9)
            for b in range(B):
                pe.matmul(work[b], sel[:, b, :], grow[:, :], start=True, stop=True).then_inc(bc_mm, 1)
            pe.wait_ge(bc_evac, B)
            with pe.Fori(0, B) as b:
                pe.wait_ge(out_ready, after(NB * b))
                transpose_h(2 * b)
                project_qk(b)
                project_v(b)
                for k in range(NMT):
                    scores(b, 0, k)
                transpose_maxima(b, 0)
                pe.wait_ge(v_ready, after(NB * b + NB))
                for t in range(NG):
                    attention(b, t)
                project_out(b)
                transpose_h(2 * b + 1)
                gate_logits(b)
                ffn(b)


def kernel(L0_attn_x, L0_attn_Wq_w, L0_attn_Wq_b, L0_attn_Wk_w, L0_attn_Wk_b, L0_attn_Wv_w, L0_attn_Wv_b,
           L0_attn_Wo_w, L0_attn_Wo_b, L0_ffn_cond, L0_ffn_mask, L0_ffn_W_shared, L0_ffn_W_expert,
           L0_ffn_W_gate, L0_ffn_bias, L0_c, L0_wmod):
    import numpy as np
    import concourse.bacc as bacc
    from concourse.bass_utils import run_bass_kernel_spmd

    def rows(a):
        return np.ascontiguousarray(a)

    def turned(a):
        return np.ascontiguousarray(np.asarray(a).T)

    def line(a):
        return rows(a).reshape(1, -1)

    arrays = {
        "x": rows(L0_attn_x), "wq_t": turned(L0_attn_Wq_w), "wk_t": turned(L0_attn_Wk_w),
        "wv_t": turned(L0_attn_Wv_w), "wo_t": turned(L0_attn_Wo_w), "ws_t": turned(L0_ffn_W_shared),
        "we_t": turned(L0_ffn_W_expert), "wgate": rows(L0_ffn_W_gate),
        "bq": turned(rows(L0_attn_Wq_b).reshape(KT, P)), "bk": turned(rows(L0_attn_Wk_b).reshape(KT, P)),
        "bv": line(L0_attn_Wv_b), "bo": line(L0_attn_Wo_b), "bf": line(L0_ffn_bias),
        "c_t": turned(L0_c), "wmod": rows(L0_wmod),
    }
    nc = bacc.Bacc("TRN2", target_bir_lowering=False, num_devices=1)
    args = {n: nc.dram_tensor(n, a.shape, mybir.dt.from_np(a.dtype), kind="ExternalInput").ap()
            for n, a in arrays.items()}
    args["out"] = nc.dram_tensor("out", (B, T, D), F32, kind="ExternalOutput").ap()
    adaln_block(nc, **args)
    r = run_bass_kernel_spmd(nc, [arrays], core_ids=[0])
    return r.results[0]["out"]
```

```python
from contextlib import ExitStack

import concourse.bass as bass
from concourse import mybir
from concourse.alu_op_type import AluOpType as ALU

ACT = mybir.ActivationFunctionType
AX = mybir.AxisListType
F32 = mybir.dt.float32
BF16 = mybir.dt.bfloat16

P = 128
B, T, D = 4, 1024, 256
H, DH = 16, 16
NB = T // P
KT = D // P
CH = 512
NC = T // CH
HG = 4
NG = H // HG
E_GATE = 7
LN_EPS = 1e-5
GATE_FLOOR = 0.25
SCORE_SCALE = 1.0 / D ** 0.5
MASKED = -3.0e38

Q_PARTS = (0, 0, 1, 1, 0, 2)
K_PARTS = (0, 1, 0, 1, 2, 0)
ROWS = DH * len(Q_PARTS)
MROWS = 3

MOD_SA, MOD_CA, MOD_GA, MOD_SB, MOD_CB, MOD_GB = range(6)


def max_tiles():
    tiles = []
    for i in range(NB):
        for half in range(2):
            keys = min((i + 1) * P - half * CH, CH)
            if keys <= 0:
                continue
            heads = max(n for n in (1, 2, 4) if n * keys <= CH)
            for h in range(0, HG, heads):
                tiles.append((i, half, h, heads, half * CH, keys))
    return tiles


def units():
    out = []
    for c in range(NC):
        for j in range((c + 1) * CH // P):
            first = max(c * CH, j * P)
            out.append((c, j, first, (c + 1) * CH - first, j * P >= c * CH))
    return out


MAX_TILES = max_tiles()
UNITS = units()
NMT, NU = len(MAX_TILES), len(UNITS)
NEXP = 2 * NU
NDIAG = sum(u[4] for u in UNITS)
NP_BUF = 3
CHUNK_END = [sum(u[0] <= c for u in UNITS) for c in range(NC)]
NSU = NG * NU

ON_ACT = ("on", "h", "qk")


def tiles_of_batch():
    at = [(0, ("v", n)) for n in range(NB // 2)]
    for t in range(NG):
        for c in range(NC):
            if (t, c) != (NG - 1, NC - 1):
                at.append((NU * t + CHUNK_END[c] + 2, ("turn", t, c)))
    at += [(WINDOWS[t][1], ("m", t)) for t in range(1, NG)]
    return at


def tiles_of_last():
    at = [(1, ("turn", NG - 1, NC - 1))]
    at += [(2 + i, ("on", i)) for i in range(NB)]
    at += [(3 + i, ("wo", i)) for i in range(NB)]
    at += [(13 + i, ("h", 1, i)) for i in range(4)]
    at += [(18, ("gate",))]
    at += [(21 + i // 2, ("ffn", i)) for i in range(NB)]
    return at


def tiles_of_next():
    at = [(24 + i // 2, ("h", 0, i)) for i in range(4)]
    at += [(26 + n + 4 * (n // 4), ("qk", n)) for n in range(8)]
    at += [(NSU - 2, ("m", 0))]
    return at


WINDOWS = {1: (0, 10), 2: (10, 22), 3: (22, 34), 0: (36, NSU - 2)}


def max_tiles_by_unit(last):
    by_unit = [[] for _ in range(NSU)]
    for t, (u0, u1) in WINDOWS.items():
        if t == 0 and last:
            continue
        cost = [x[3] * x[5] for x in MAX_TILES]
        widths = [UNITS[u % NU][3] for u in range(u0, u1)]
        done = k = 0
        for u in range(u0, u1):
            share = sum(cost) * sum(widths[:u + 1 - u0]) / sum(widths)
            while k < NMT and done < share - 1e-9:
                done += cost[k]
                by_unit[u].append(("score", t, k))
                k += 1
        assert k == NMT
    return by_unit


def step_plan(kind):
    tiles = tiles_of_batch()
    local = []
    if kind != "first":
        tiles += tiles_of_last()
        local += [(11, ("aggregate", 1)), (12, ("normalise", 1)), (19, ("gate_soft",)), (20, ("gate_top",))]
    local += [(24, ("scale",)), (27, ("bias_x1",))]
    if kind != "last":
        tiles += tiles_of_next()
        local += [(20, ("aggregate", 0)), (22, ("normalise", 0))]
        local += [(27 + n + 4 * (n // 4), ("first_part", n)) for n in range(8)]
        local += [(28 + n + 4 * (n // 4), ("second_part", n)) for n in range(8)]
    scores = max_tiles_by_unit(kind == "last")
    plan = []
    for u in range(NSU):
        plan.append(("attend", u // NU, u % NU))
        mine = [x for at, x in sorted(tiles, key=lambda y: y[0]) if at == u]
        rest = scores[u]
        for n, x in enumerate(mine):
            k = -(-len(rest) // (len(mine) - n + 1))
            plan += [x] + rest[:k]
            rest = rest[k:]
        plan += rest
        plan += [("split_max", t) for t, w in WINDOWS.items() if w[1] - 1 == u and scores[u][-1:] and scores[u][-1][1] == t]
        plan += [x for at, x in local if at == u]
        if u:
            plan.append(("weigh", (u - 1) // NU, (u - 1) % NU))
    plan.append(("weigh", NG - 1, NU - 1))
    return plan


def start_plan():
    plan = [("aggregate", 0), ("normalise", 0)] + [("h", 0, i) for i in range(4)]
    for n in range(10):
        plan += [("qk", n)] if n < 8 else []
        parts = [("first_part", n - 1)] if 1 <= n <= 8 else []
        parts += [("second_part", n - 2)] if n >= 2 else []
        plan += parts[::-1] if n == 5 else parts
    return plan + [("score", 0, k) for k in range(NMT)] + [("split_max", 0), ("m", 0)]


def end_plan():
    plan = [("turn", NG - 1, NC - 1)]
    for i in range(NB + 1):
        plan += [("on", i)] if i < NB else []
        plan += [("wo", i - 1)] if i else []
    plan += [("aggregate", 1), ("normalise", 1)] + [("h", 1, i) for i in range(4)]
    return plan + [("gate",), ("gate_soft",), ("gate_top",)] + [("ffn", i) for i in range(NB)]


TILE_KINDS = ("v", "turn", "on", "wo", "h", "gate", "ffn", "qk", "m")


class Tiles:

    def __init__(self, plan):
        self.order = [x for x in plan if x[0] in TILE_KINDS]
        self.index = {x: n for n, x in enumerate(self.order)}
        self.all, self.act = len(self.order), sum(x[0] in ON_ACT for x in self.order)
        self.dve = self.all - self.act

    def taken(self, tile):
        upto = self.order[:self.index[tile] + 1]
        on_act = tile[0] in ON_ACT
        return on_act, sum((x[0] in ON_ACT) == on_act for x in upto)


START, END = start_plan(), end_plan()
STEPS = {kind: step_plan(kind) for kind in ("first", "middle", "last")}
TILES = {"start": Tiles(START), "end": Tiles(END), **{k: Tiles(p) for k, p in STEPS.items()}}


def counts_before(kind, b):
    start, first, middle, last = (TILES[k] for k in ("start", "first", "middle", "last"))

    def count(what):
        n = {"start": 0, "first": what(start)}
        n["middle"] = (b - 1) * what(middle) + what(start) + what(first)
        n["last"] = (B - 2) * what(middle) + what(start) + what(first)
        n["end"] = n["last"] + what(last)
        return n[kind]

    if kind != "middle":
        b = 1
    return count(lambda t: t.all), count(lambda t: t.act), count(lambda t: t.dve)


def adaln_block(nc, x, wq_t, wk_t, wv_t, wo_t, ws_t, we_t, wgate, bq, bk, bv, bo, bf, c_t, wmod, out):
    with ExitStack() as ctx:
        def sb(name, shape, dt=F32):
            return ctx.enter_context(nc.sbuf_tensor(name, shape, dt))

        def pb(name, shape, dt=F32):
            return ctx.enter_context(nc.psum_tensor(name, shape, dt))

        def sem(name):
            return ctx.enter_context(nc.semaphore(name))

        counted = []

        def counted_sem(name):
            counted.append(sem(name))
            return counted[-1]

        def after(n):
            return n + 1

        wq = sb("wq", [P, KT, D])
        wk = sb("wk", [P, KT, D])
        wv = sb("wv", [P, KT, D])
        wo = sb("wo", [P, KT, D])
        wse = sb("wse", [P, KT, 2 * D])
        wg = sb("wg", [P, KT, E_GATE])
        wo_g = sb("wo_g", [P, KT, D])
        wse_g = sb("wse_g", [P, KT, 2 * D])
        bqk = sb("bqk", [P, 2, KT])
        bv_bc = sb("bv_bc", [P, D])
        bob_bc = sb("bob_bc", [P, 2, D])
        gate_bc = sb("gate_bc", [P, B, 2, D])
        gbias = sb("gbias", [P, 2, D])
        modc = sb("modc", [P, 6, KT, B])
        ct = sb("ct", [P, KT, B])
        ect = sb("ect", [P, KT, B])
        silu = sb("silu", [P, KT, B])
        grow = sb("grow", [B, 2 * D])
        sel = sb("sel", [B, B, P])
        ident = sb("ident", [P, P])
        ident_b = sb("ident_b", [P, P], BF16)
        mask_b = sb("mask_b", [P, P], BF16)
        nhalf = sb("nhalf", [P, NB])
        xs = sb("xs", [P, NB, D])
        xn = sb("xn", [P, NB, D])
        ht = sb("ht", [P, KT, T])
        stats = sb("stats", [P, NB, 6])
        mv = sb("mv", [P, NB, 2])
        ve = sb("ve", [P, NB])
        rstd = sb("rstd", [P, NB])
        stage = sb("stage", [P, 2, CH])
        gsign, gabs = stage[0:B, 0, :], stage[0:B, 1, :]
        rest = sb("rest", [P, 2, CH])
        parts = sb("parts", [P, 2, 3, T], BF16)
        wm = parts[:, :, :, :].rearrange("p w r n -> p (w r n)").bitcast(F32).rearrange("p (k n) -> p k n", k=KT)
        v = sb("v", [P, NB, H, DH + 1])
        qs = [sb(f"qs{t}", [ROWS + MROWS, HG, T], BF16) for t in range(NG)]
        ks = [sb(f"ks{t}", [ROWS + MROWS, HG, T], BF16) for t in range(NG)]
        mpart = sb("mpart", [P, HG, NB, 2])
        mx = sb("mx", [P, HG * NB])
        mrest = sb("mrest", [P, HG * NB])
        m3 = sb("m3", [P, MROWS, HG * NB], BF16)
        mrow = sb("mrow", [MROWS * HG * NB, P], BF16)
        probs = [sb(f"probs{i}", [P, HG, CH]) for i in range(NP_BUF)]
        ot = sb("ot", [P, 2, CH])
        rec = sb("rec", [P, CH // P, HG])
        on = sb("on", [P, NB, H, DH])
        ont = sb("ont", [P, 2, KT, P])
        x1 = sb("x1", [P, NB, D])
        logit = sb("logit", [P, NB, 8])
        lmax = sb("lmax", [P, NB])
        lexp = sb("lexp", [P, NB, 8])
        lsum = sb("lsum", [P, NB])
        score = sb("score", [P, NB, 8])
        top8 = sb("top8", [P, NB, 8])
        tsum = sb("tsum", [P, NB])
        wtop = sb("wtop", [P, NB, 2])
        wsum = sb("wsum", [P, NB])
        y = sb("y", [P, 2, D])

        ps_t = [pb(f"ps_t{i}", [P, 2, CH]) for i in range(2)]
        work = [ps_t[i // 2][:, i % 2, :] for i in range(4)]
        ps_m = [pb(f"ps_m{i}", [P, CH]) for i in range(2)]
        ps_o = pb("ps_o", [P, CH])
        ps_x = pb("ps_x", [P, CH])
        scratch = nc.dram_tensor("parts_scratch", [B, 2, 3, D, T], BF16, kind="Internal").ap()

        w_loaded = sem("w_loaded")
        x_loaded = counted_sem("x_loaded")
        pool_const = sem("pool_const")
        dve_const = sem("dve_const")
        c_exp = sem("c_exp")
        silu_step = sem("silu_step")
        mod_mm = sem("mod_mm")
        mod_step = sem("mod_step")
        gate_ready = sem("gate_ready")
        bc_mm = sem("bc_mm")
        bc_evac = sem("bc_evac")
        gbias_ready = counted_sem("gbias_ready")
        w_scaled = counted_sem("w_scaled")
        x1_loaded = counted_sem("x1_loaded")
        tile_mm = counted_sem("tile_mm")
        tile_act = counted_sem("tile_act")
        tile_dve = counted_sem("tile_dve")
        ln_stats = [counted_sem(f"ln{s}_stats") for s in range(2)]
        ln_mv = [counted_sem(f"ln{s}_mv") for s in range(2)]
        ln_rstd = [counted_sem(f"ln{s}_rstd") for s in range(2)]
        xn_ready = [counted_sem(f"xn{s}_ready") for s in range(2)]
        p1_ready = counted_sem("p1_ready")
        r_ready = counted_sem("r_ready")
        p2_ready = counted_sem("p2_ready")
        p3_ready = counted_sem("p3_ready")
        parts_stored = [counted_sem(f"parts_stored{i}") for i in range(KT)]
        stack_loaded = [counted_sem(f"stack_loaded{t}") for t in range(NG)]
        mrow_loaded = [counted_sem(f"mrow_loaded{t}") for t in range(NG)]
        v_ready = counted_sem("v_ready")
        s_mm = counted_sem("s_mm")
        s_red = counted_sem("s_red")
        m_step = counted_sem("m_step")
        m3_ready = counted_sem("m3_ready")
        st_mm = counted_sem("st_mm")
        exp_done = counted_sem("exp_done")
        diag_done = counted_sem("diag_done")
        pv_done = counted_sem("pv_done")
        po_evac = counted_sem("po_evac")
        rec_ready = counted_sem("rec_ready")
        x1_biased = counted_sem("x1_biased")
        x1b_ready = counted_sem("x1b_ready")
        g_step = counted_sem("g_step")
        g_exp = counted_sem("g_exp")
        y_ready = counted_sem("y_ready")
        out_stored = counted_sem("out_stored")

        N_WLOADS = 14
        G_STEPS = 6 + NB + 4

        xv = x.rearrange("b (n p) d -> b p n d", p=P)
        ov = out.rearrange("b (n p) d -> b p n d", p=P)

        def apart(engine):
            engine.nop(nofuse=True)

        def tile_wait(engine, kind, b, tile):
            engine.wait_ge(tile_mm, after(counts_before(kind, b)[0] + TILES[kind].index[tile] + 1))

        def bank_of(kind, tile):
            return work[TILES[kind].index[tile] % 4] if kind in ("start", "end") else ps_x[:, :]

        def score_group(b, t):
            return NG * (b + 1) if t == 0 else NG * b + t

        def steps(engine, part):
            part("start", 0)
            part("first", 0)
            with engine.Fori(1, B - 1) as b:
                part("middle", b)
            part("last", B - 1)
            part("end", B)

        def plan_of(kind):
            return {"start": START, "end": END}.get(kind) or STEPS[kind]

        block = ctx.enter_context(nc.Block())

        @block.sync
        def _(sp):
            def at_batch(b):
                return bass.ds(b, 1)

            def load_x(b, dst, loaded):
                sp.dma_start(dst[:, :, :], xv[at_batch(b)].rearrange("o p n d -> (o p) n d")).then_inc(loaded, 16)

            def store_parts(b, mt):
                for which in range(2):
                    sp.wait_ge(p3_ready, after(8 * b + 4 * mt + 2 * which + 2))
                    for part in range(3):
                        sp.dma_start(scratch[at_batch(b), which, part, mt * P:(mt + 1) * P, :]
                                     .rearrange("o p n -> (o p) n"),
                                     parts[:, which, part, :]).then_inc(parts_stored[mt], 16)

            def load_stacks(b, t, later):
                sp.wait_ge(parts_stored[t // 2], after(96 * b + 96))
                if later:
                    apart(sp)
                    sp.wait_ge(st_mm, after(NEXP * (NG * (b - 1) + t + 1)))
                f0 = t * HG * DH
                for which, dst, order in ((0, qs, Q_PARTS), (1, ks, K_PARTS)):
                    for r, part in enumerate(order):
                        src = scratch[at_batch(b), which, part, f0:f0 + HG * DH, :]
                        sp.dma_start(dst[t][r * DH:(r + 1) * DH, :, :],
                                     src.rearrange("o (h d) n -> (o d) h n", d=DH)
                                     ).then_inc(stack_loaded[t], 16)

            def taken(kind, b, tile):
                sp.wait_ge(tile_dve, after(counts_before(kind, b)[2] + TILES[kind].taken(tile)[1]))

            def load_rows(kind, b, batch, t):
                taken(kind, b, ("m", t))
                n = HG * NB
                for r in range(MROWS):
                    sp.dma_start(qs[t][ROWS + r:ROWS + r + 1, :, :].rearrange("o h (i q) -> o (h i) q", q=P),
                                 mrow[r * n:(r + 1) * n, :]).then_inc(mrow_loaded[t], 16)

            def store_out(kind, b, batch, half):
                n0 = half * NB // 2
                taken(kind, b, ("ffn", n0 + NB // 2 - 1))
                sp.dma_start(ov[at_batch(batch), :, n0:n0 + NB // 2, :].rearrange("o p n d -> (o p) n d"),
                             x1[:, n0:n0 + NB // 2, :]).then_inc(out_stored, 16)

            def part(kind, b):
                if kind == "start":
                    store_parts(0, 0)
                    load_stacks(0, 0, False)
                    store_parts(0, 1)
                    load_stacks(0, 1, False)
                    load_stacks(0, 2, False)
                    load_rows("start", 0, 0, 0)
                    return
                if kind == "end":
                    store_out("end", B, B - 1, 0)
                    store_out("end", B, B - 1, 1)
                    return
                last, this, next_ = b - 1, b, b + 1
                if kind == "middle":
                    last, next_ = sp.snap(b - 1), sp.snap(b + 1)
                load_stacks(this, 3, kind != "first")
                if kind != "last":
                    sp.wait_ge(xn_ready[0], after(NB * this + NB))
                    load_x(next_, xs, x_loaded)
                load_rows(kind, b, this, 1)
                if kind != "first":
                    store_out(kind, b, last, 0)
                load_rows(kind, b, this, 2)
                if kind != "first":
                    store_out(kind, b, last, 1)
                    sp.wait_ge(out_stored, after(32 * this))
                    load_x(this, x1, x1_loaded)
                else:
                    load_x(this, x1, x1_loaded)
                if kind != "last":
                    store_parts(next_, 0)
                    load_stacks(next_, 0, True)
                    load_stacks(next_, 1, True)
                load_rows(kind, b, this, 3)
                if kind != "last":
                    store_parts(next_, 1)
                    load_stacks(next_, 2, True)
                    load_rows(kind, b, next_, 0)

            sp.dma_start(xs[:, :, :], xv[0]).then_inc(x_loaded, 16)
            for s in counted:
                sp.sem_inc(s, 1)
            for dst, src in ((wq, wq_t), (wk, wk_t), (wv, wv_t), (wo, wo_t)):
                sp.dma_start(dst[:, :, :], src.rearrange("(k p) n -> p k n", p=P)).then_inc(w_loaded, 16)
            sp.dma_start(wse[:, :, 0:D], ws_t.rearrange("(k p) n -> p k n", p=P)).then_inc(w_loaded, 16)
            sp.dma_start(wse[:, :, D:2 * D], we_t.rearrange("(k p) n -> p k n", p=P)).then_inc(w_loaded, 16)
            sp.dma_start(wg[:, :, :], wgate.rearrange("(k p) n -> p k n", p=P)).then_inc(w_loaded, 16)
            sp.dma_start(bqk[:, 0, :], bq).then_inc(w_loaded, 16)
            sp.dma_start(bqk[:, 1, :], bk).then_inc(w_loaded, 16)
            for dst, src in ((bv_bc[:, :], bv), (bob_bc[:, 0, :], bo), (bob_bc[:, 1, :], bf)):
                sp.dma_start(dst, src.to_broadcast([P, D])).then_inc(w_loaded, 16)
            sp.dma_start(ct[:, :, :], c_t.rearrange("(k p) n -> p k n", p=P)).then_inc(w_loaded, 16)
            sp.dma_start(wm[:, :, :], wmod.rearrange("(k p) n -> p k n", p=P)).then_inc(w_loaded, 16)
            steps(sp, part)
            sp.wait_ge(out_stored, after(2 * 16 * B))
            for mt in range(KT):
                sp.wait_ge(parts_stored[mt], after(96 * B))

        @block.gpsimd
        def _(pool):
            def consts():
                pool.memset(ident[:, :], 0.0).then_inc(pool_const, 1)
                pool.memset(ident_b[:, :], 0.0).then_inc(pool_const, 1)
                pool.memset(mask_b[:, :], 0.0).then_inc(pool_const, 1)
                pool.memset(sel[:, :, :], 0.0).then_inc(pool_const, 1)
                pool.memset(nhalf[:, :], -0.5).then_inc(pool_const, 1)
                pool.wait_ge(pool_const, 5)
                for m in (ident, ident_b):
                    pool.affine_select(out=m[:, :], in_=m[:, :], compare_op=ALU.not_equal, fill=1.0, base=0,
                                       pattern=[[-1, P]], channel_multiplier=1).then_inc(pool_const, 1)
                pool.affine_select(out=mask_b[:, :], in_=mask_b[:, :], compare_op=ALU.is_ge, fill=MASKED,
                                   base=0, pattern=[[-1, P]], channel_multiplier=1).then_inc(pool_const, 1)
                pool.affine_select(out=sel[:, :, :], in_=sel[:, :, :], compare_op=ALU.not_equal, fill=1.0,
                                   base=0, pattern=[[-1, B], [0, P]], channel_multiplier=1).then_inc(pool_const, 1)

            def scale_weights(kind, b):
                if kind != "first":
                    pool.wait_ge(tile_dve, after(counts_before(kind, b)[2] + TILES[kind].taken(("ffn", NB - 1))[1]))
                ga = gate_bc[:, bass.ds(b, 1), 0, :]
                gb = gate_bc[:, bass.ds(b, 1), 1, :]
                if kind != "first":
                    pool.wait_ge(x1b_ready, after(NB * b))
                for e, g in enumerate((ga, gb)):
                    pool.tensor_tensor(gbias[:, e:e + 1, :], bob_bc[:, e:e + 1, :], g, ALU.mult).then_inc(gbias_ready, 1)
                for k in range(KT):
                    pool.tensor_tensor(wo_g[:, k:k + 1, :], wo[:, k:k + 1, :], ga, ALU.mult).then_inc(w_scaled, 1)
                    for e in range(2):
                        pool.tensor_tensor(wse_g[:, k:k + 1, e * D:(e + 1) * D], wse[:, k:k + 1, e * D:(e + 1) * D],
                                           gb, ALU.mult).then_inc(w_scaled, 1)

            def rstd_of(s, b):
                pool.wait_ge(ln_mv[s], after(NB * b + NB))
                apart(pool)
                pool.tensor_scalar(ve[:, :], mv[:, :, 1], LN_EPS, None, ALU.add).then_inc(ln_rstd[s], 1)
                pool.wait_ge(ln_rstd[s], after(2 * b + 1))
                pool.tensor_tensor(rstd[:, :], ve[:, :], nhalf[:, :], ALU.pow).then_inc(ln_rstd[s], 1)

            def add_bias(b, which, ready):
                for i in range(NB):
                    pool.tensor_tensor(x1[:, i, :], x1[:, i, :], gbias[:, which, :], ALU.add).then_inc(ready, 1)

            def rest_of(b, n):
                mt, which, c = n // 4, n // 2 % 2, n % 2
                pool.wait_ge(p1_ready, after(8 * b + n + 1))
                pool.wait_ge(p3_ready, after(8 * b + max(n - 1, 0)))
                pool.tensor_tensor(rest[:, n % 2, :], stage[:, n % 2, :],
                                   parts[:, which, 0, c * CH:(c + 1) * CH], ALU.subtract).then_inc(r_ready, 1)

            def third_part(b, n):
                mt, which, c = n // 4, n // 2 % 2, n % 2
                pool.wait_ge(p2_ready, after(8 * b + n + 1))
                pool.tensor_tensor(parts[:, which, 2, c * CH:(c + 1) * CH], rest[:, n % 2, :],
                                   parts[:, which, 1, c * CH:(c + 1) * CH], ALU.subtract).then_inc(p3_ready, 1)

            def mask_diagonal(b, t, u):
                pool.wait_ge(exp_done, after(NEXP * (NG * b + t) + 2 * u + 2))
                pr = probs[u % NP_BUF][:, :, 0:P]
                apart(pool)
                pool.affine_select(out=pr, in_=pr, compare_op=ALU.is_ge, fill=0.0, base=0,
                                   pattern=[[0, HG], [1, P]], channel_multiplier=-1).then_inc(diag_done, 1)

            def part(kind, b):
                nxt = 0 if kind == "start" else b + 1
                for what, *arg in plan_of(kind):
                    if what == "attend" and UNITS[arg[1]][4]:
                        mask_diagonal(b, *arg)
                    elif what == "aggregate":
                        s, = arg
                        rstd_of(s, b - 1 if s else nxt)
                    elif what == "normalise" and arg[0] == 1:
                        pool.wait_ge(xn_ready[1], after(NB * b))
                        add_bias(b - 1, 1, x1b_ready)
                    elif what == "scale":
                        scale_weights(kind, b)
                    elif what == "bias_x1":
                        pool.wait_ge(x1_loaded, after(16 * b + 16))
                        pool.wait_ge(gbias_ready, after(2 * b + 2))
                        add_bias(b, 0, x1_biased)
                    elif what == "first_part":
                        rest_of(nxt, *arg)
                    elif what == "second_part":
                        third_part(nxt, *arg)

            consts()
            pool.wait_ge(bc_evac, B + 1)
            pool.wait_ge(w_loaded, 16 * N_WLOADS)
            steps(pool, part)

        @block.scalar
        def _(act):
            def modulate(kind, b, batch, s, i):
                shift, scale = (MOD_SB, MOD_CB) if s else (MOD_SA, MOD_CA)
                k, ch = i // 2, i % 2
                tile_wait(act, kind, b, ("h", s, i))
                apart(act)
                act.activation(ht[:, k, ch * CH:(ch + 1) * CH], bank_of(kind, ("h", s, i)), ACT.Identity,
                               bias=modc[:, shift, k, bass.ds(batch, 1)],
                               scale=modc[:, scale, k, bass.ds(batch, 1)]).then_inc(tile_act, 1)

            def stage_qk(kind, b, batch, n):
                mt, which = n // 4, n // 2 % 2
                tile_wait(act, kind, b, ("qk", n))
                act.wait_ge(r_ready, after(8 * batch + max(n - 1, 0)))
                act.activation(stage[:, n % 2, :], bank_of(kind, ("qk", n)), ACT.Identity,
                               bias=bqk[:, which, mt:mt + 1]).then_inc(tile_act, 1)

            def exps(kind, b, t, u):
                width = UNITS[u][3]
                for pr in range(2):
                    act.wait_ge(st_mm, after(NEXP * (NG * b + t) + 2 * u + pr + 1))
                    if pr == 0 and not (kind == "first" and NU * t + u < NP_BUF):
                        act.wait_ge(pv_done, after(NSU * b + NU * t + u - NP_BUF + 1))
                    act.activation(probs[u % NP_BUF][:, 2 * pr:2 * pr + 2, 0:width], ps_t[pr][:, :, 0:width],
                                   ACT.Exp, scale=SCORE_SCALE).then_inc(exp_done, 1)

            def part(kind, b):
                nxt = 0 if kind == "start" else b + 1
                for what, *arg in plan_of(kind):
                    if what == "attend":
                        exps(kind, b, *arg)
                    elif what == "h":
                        s, i = arg
                        modulate(kind, b, b - 1 if s else nxt, s, i)
                    elif what == "qk":
                        stage_qk(kind, b, nxt, *arg)
                    elif what == "on":
                        i, = arg
                        tile_wait(act, kind, b, ("on", i))
                        act.activation(ont[:, i % 2, :, :],
                                       bank_of(kind, ("on", i))[:, 0:D].rearrange("p (k n) -> p k n", k=KT),
                                       ACT.Copy).then_inc(tile_act, 1)
                    elif what == "gate_soft":
                        act.wait_ge(g_step, after(G_STEPS * (b - 1) + 3))
                        act.activation(lexp[:, :, :], lexp[:, :, :], ACT.Exp).then_inc(g_exp, 1)

            act.wait_ge(w_loaded, 16 * N_WLOADS)
            act.activation(ect[:, :, :], ct[:, :, :], ACT.Exp, scale=-1.0).then_inc(c_exp, 1)
            act.wait_ge(mod_step, 3)
            steps(act, part)

        @block.vector
        def _(dve):
            def spread(a, n):
                return a[:, :].rearrange("p (i o) -> p i o", o=1).to_broadcast([P, NB, n])

            def statistics(s, src, i):
                dve.bn_stats(stats[:, i, :], src[:, i, :]).then_inc(ln_stats[s], 1)

            def aggregate(s, batch):
                if s == 0:
                    dve.wait_ge(x_loaded, after(16 * batch + 16))
                    for i in range(NB):
                        statistics(0, xs, i)
                for i in range(NB):
                    dve.wait_ge(ln_stats[s], after(NB * batch + i + 1))
                    apart(dve)
                    dve.bn_aggr(mv[:, i, :], stats[:, i, :]).then_inc(ln_mv[s], 1)

            def normalise(kind, b, s, batch, src):
                dve.wait_ge(ln_rstd[s], after(2 * batch + 2))
                before = counts_before(kind, b)[0]
                if kind in ("middle", "last") and s == 0:
                    before = before + TILES[kind].index[("h", 1, 3)] + 1
                if kind != "start":
                    dve.wait_ge(tile_mm, after(before))
                for i in range(NB):
                    dve.tensor_scalar(xn[:, i, :], src[:, i, :], mv[:, i, 0:1], rstd[:, i:i + 1],
                                      ALU.subtract, ALU.mult).then_inc(xn_ready[s], 1)

            def first_part(kind, b, batch, n):
                mt, which, c = n // 4, n // 2 % 2, n % 2
                if n == 4:
                    dve.wait_ge(parts_stored[0], after(96 * batch + 96))
                elif n == 0 and kind != "start":
                    dve.wait_ge(parts_stored[1], after(96 * batch))
                dve.wait_ge(tile_act, after(counts_before(kind, b)[1] + TILES[kind].taken(("qk", n))[1]))
                dve.tensor_copy(parts[:, which, 0, c * CH:(c + 1) * CH],
                                stage[:, n % 2, :]).then_inc(p1_ready, 1)

            def second_part(batch, n):
                mt, which, c = n // 4, n // 2 % 2, n % 2
                dve.wait_ge(r_ready, after(8 * batch + n + 1))
                dve.tensor_copy(parts[:, which, 1, c * CH:(c + 1) * CH],
                                rest[:, n % 2, :]).then_inc(p2_ready, 1)

            def values(kind, b, n):
                tile_wait(dve, kind, b, ("v", n))
                for i in range(2):
                    ins = dve.tensor_tensor(v[:, 2 * n + i, :, 0:DH],
                                            bank_of(kind, ("v", n))[:, i * D:(i + 1) * D]
                                            .rearrange("p (h d) -> p h d", d=DH),
                                            bv_bc[:, :].rearrange("p (h d) -> p h d", d=DH), ALU.add)
                ins.then_inc(tile_dve, 1)

            def maximum(b, t, k):
                i, half, h0, heads, key0, keys = MAX_TILES[k]
                n = NMT * score_group(b, t) + k
                dve.wait_ge(s_mm, after(n + 1))
                dve.tensor_reduce(mpart[:, h0:h0 + heads, i, half],
                                  ps_m[k % 2][:, 0:heads * keys].rearrange("p (h n) -> p h n", h=heads),
                                  AX.X, ALU.max).then_inc(s_red, 1)

            def split_maxima(b, t):
                g = score_group(b, t)
                dve.wait_ge(s_red, after(NMT * g + NMT))
                dve.tensor_reduce(mx[:, :], mpart[:, :, :, :].rearrange("p h i a -> p (h i) a"),
                                  AX.X, ALU.max).then_inc(m_step, 1)
                dve.wait_ge(m_step, after(4 * g + 1))
                dve.tensor_scalar(m3[:, 0, :], mx[:, :], -1.0, None, ALU.mult).then_inc(m_step, 1)
                dve.wait_ge(m_step, after(4 * g + 2))
                dve.scalar_tensor_tensor(out=mrest[:, :], in0=mx[:, :], scalar=-1.0, in1=m3[:, 0, :],
                                         op0=ALU.mult, op1=ALU.subtract).then_inc(m_step, 1)
                dve.wait_ge(m_step, after(4 * g + 3))
                dve.tensor_copy(m3[:, 1, :], mrest[:, :]).then_inc(m_step, 1)
                dve.wait_ge(m_step, after(4 * g + 4))
                dve.tensor_tensor(m3[:, 2, :], mrest[:, :], m3[:, 1, :], ALU.subtract).then_inc(m3_ready, 1)

            def maxima_rows(kind, b, t):
                tile_wait(dve, kind, b, ("m", t))
                if kind != "start":
                    dve.wait_ge(mrow_loaded[(t - 1) % NG], after(48 * b + 48))
                bank = bank_of(kind, ("m", t))[:, 0:P // 2].bitcast(BF16)
                dve.tensor_copy(mrow[:, :], bank[0:MROWS * HG * NB, :]).then_inc(tile_dve, 1)

            def chunk_out(b, t, c):
                dve.wait_ge(pv_done, after(NU * (NG * b + t) + CHUNK_END[c]))
                dve.tensor_copy(ot[:, c, :], ps_o[:, :]).then_inc(po_evac, 1)

            def turn(kind, b, batch, t, c):
                tile_wait(dve, kind, b, ("turn", t, c))
                bank = bank_of(kind, ("turn", t, c))
                dve.reciprocal(rec[:, :, :].rearrange("p k h -> p (k h)"),
                               bank.rearrange("p (n r) -> p n r", r=2 * DH)[:, :, DH]).then_inc(rec_ready, 1)
                dve.wait_ge(rec_ready, after(NC * (NG * batch + t) + c + 1))
                k = CH // P
                for j in range(k):
                    ins = dve.tensor_tensor(on[:, k * c + j, HG * t:HG * t + HG, :],
                                            bank[:, j * P:(j + 1) * P].rearrange("p (h r) -> p h r", h=HG)[:, :, 0:DH],
                                            rec[:, j, :].rearrange("p (h o) -> p h o", o=1).to_broadcast([P, HG, DH]),
                                            ALU.mult)
                ins.then_inc(tile_dve, 1)

            def output(kind, b, batch, i):
                tile_wait(dve, kind, b, ("wo", i))
                if i == 0:
                    dve.wait_ge(x1_biased, after(NB * batch + NB))
                dve.tensor_tensor(x1[:, i, :], bank_of(kind, ("wo", i))[:, 0:D], x1[:, i, :],
                                  ALU.add).then_inc(tile_dve, 1)
                dve.wait_ge(tile_dve, after(counts_before(kind, b)[2] + TILES[kind].taken(("wo", i))[1]))
                statistics(1, x1, i)

            def linker(batch, done):
                step = [done]

                def link(ins):
                    step[0] += 1
                    ins.then_inc(g_step, 1)
                    dve.wait_ge(g_step, after(G_STEPS * batch + step[0]))

                return link

            def take_logits(kind, b):
                tile_wait(dve, kind, b, ("gate",))
                dve.tensor_copy(logit[:, :, 0:E_GATE],
                                bank_of(kind, ("gate",))[:, 0:8 * NB]
                                .rearrange("p (i e) -> p i e", e=8)[:, :, 0:E_GATE]).then_inc(tile_dve, 1)

            def gate_softmax(kind, b, batch):
                link = linker(batch, 0)
                dve.wait_ge(tile_dve, after(counts_before(kind, b)[2] + TILES[kind].taken(("gate",))[1]))
                link(dve.tensor_reduce(lmax[:, :], logit[:, :, :], AX.X, ALU.max))
                dve.tensor_tensor(lexp[:, :, :], logit[:, :, :], spread(lmax, 8), ALU.subtract).then_inc(g_step, 2)

            def gate_top(batch):
                link = linker(batch, 3)
                dve.wait_ge(g_exp, after(batch + 1))
                link(dve.tensor_reduce(lsum[:, :], lexp[:, :, :], AX.X, ALU.add))
                link(dve.reciprocal(lsum[:, :], lsum[:, :]))
                link(dve.tensor_tensor(score[:, :, :], lexp[:, :, :], spread(lsum, 8), ALU.mult))
                for i in range(NB):
                    apart(dve)
                    link(dve.max(top8[:, i, :], score[:, i, :]))
                link(dve.tensor_reduce(tsum[:, :], top8[:, :, 0:2], AX.X, ALU.add))
                link(dve.reciprocal(tsum[:, :], tsum[:, :]))
                link(dve.tensor_tensor(wtop[:, :, :], top8[:, :, 0:2], spread(tsum, 2), ALU.mult))
                link(dve.tensor_reduce(wsum[:, :], wtop[:, :, :], AX.X, ALU.add))

            def finish(kind, b, batch, i):
                if i == 0:
                    dve.wait_ge(x1b_ready, after(NB * batch + NB))
                tile_wait(dve, kind, b, ("ffn", i))
                bank = bank_of(kind, ("ffn", i))
                dve.scalar_tensor_tensor(out=y[:, i % 2, :], in0=bank[:, D:2 * D], scalar=wsum[:, i:i + 1],
                                         in1=x1[:, i, :], op0=ALU.mult, op1=ALU.add).then_inc(y_ready, 1)
                dve.wait_ge(y_ready, after(NB * batch + i + 1))
                dve.tensor_tensor(x1[:, i, :], bank[:, 0:D], y[:, i % 2, :], ALU.add).then_inc(tile_dve, 1)

            def modulation():
                dve.wait_ge(c_exp, 1)
                dve.tensor_scalar(ect[:, :, :], ect[:, :, :], 1.0, None, ALU.add).then_inc(silu_step, 1)
                dve.wait_ge(silu_step, 1)
                dve.reciprocal(ect[:, :, :], ect[:, :, :]).then_inc(silu_step, 1)
                dve.wait_ge(silu_step, 2)
                dve.tensor_tensor(silu[:, :, :], ct[:, :, :], ect[:, :, :], ALU.mult).then_inc(silu_step, 1)
                dve.wait_ge(mod_mm, 2)
                dve.tensor_copy(modc[:, :, :, :].rearrange("p m k b -> p (m k b)"),
                                ps_x[:, 0:6 * KT * B]).then_inc(mod_step, 1)
                dve.wait_ge(mod_step, 1)
                for m in (MOD_CA, MOD_CB):
                    dve.tensor_scalar(modc[:, m, :, :], modc[:, m, :, :], 1.0, None, ALU.add).then_inc(mod_step, 1)
                dve.tensor_copy(grow[:, :], ps_o[0:B, :]).then_inc(mod_step, 1)
                dve.wait_ge(mod_step, 4)
                dve.tensor_scalar(gsign, grow[:, :], 0.0, 2.0, ALU.is_ge, ALU.mult).then_inc(mod_step, 1)
                dve.scalar_tensor_tensor(out=gabs, in0=grow[:, :], scalar=-1.0, in1=grow[:, :],
                                         op0=ALU.mult, op1=ALU.max).then_inc(mod_step, 1)
                dve.wait_ge(mod_step, 6)
                dve.tensor_scalar(gabs, gabs, GATE_FLOOR, None, ALU.max).then_inc(mod_step, 1)
                dve.wait_ge(mod_step, 7)
                dve.scalar_tensor_tensor(out=grow[:, :], in0=gsign, scalar=-1.0, in1=gabs,
                                         op0=ALU.add, op1=ALU.mult).then_inc(gate_ready, 1)
                dve.wait_ge(gate_ready, 1)
                dve.memset(ps_o[:, :], 0.0).then_inc(bc_evac, 1)
                for b in range(B):
                    dve.wait_ge(bc_mm, b + 1)
                    dve.tensor_copy(gate_bc[:, b, :, :].rearrange("p a d -> p (a d)"), work[b]).then_inc(bc_evac, 1)

            def part(kind, b):
                nxt = 0 if kind == "start" else b + 1
                last = b - 1
                for what, *arg in plan_of(kind):
                    if what == "score":
                        maximum(-1 if kind == "start" else b, arg[0], arg[1])
                    elif what == "split_max":
                        split_maxima(-1 if kind == "start" else b, *arg)
                    elif what == "m":
                        maxima_rows(kind, b, *arg)
                    elif what == "weigh":
                        t, u = arg
                        for c in range(NC):
                            if u + 1 == CHUNK_END[c]:
                                chunk_out(b, t, c)
                    elif what == "v":
                        values(kind, b, *arg)
                    elif what == "turn":
                        turn(kind, b, last if tuple(arg) == (NG - 1, NC - 1) else b, *arg)
                    elif what == "wo":
                        output(kind, b, last, *arg)
                    elif what == "aggregate":
                        aggregate(arg[0], last if arg[0] else nxt)
                    elif what == "normalise":
                        s, = arg
                        normalise(kind, b, s, last if s else nxt, x1 if s else xs)
                    elif what == "gate":
                        take_logits(kind, b)
                    elif what == "gate_soft":
                        gate_softmax(kind, b, last)
                    elif what == "gate_top":
                        gate_top(last)
                    elif what == "ffn":
                        finish(kind, b, last, *arg)
                    elif what == "first_part":
                        first_part(kind, b, nxt, *arg)
                    elif what == "second_part":
                        second_part(nxt, *arg)

            dve.memset(v[:, :, :, DH:DH + 1], 1.0).then_inc(dve_const, 1)
            dve.memset(mpart[:, :, :, :], MASKED).then_inc(dve_const, 1)
            dve.memset(logit[:, :, :], MASKED).then_inc(dve_const, 1)
            for t in range(NG):
                dve.memset(ks[t][ROWS:ROWS + MROWS, :, :], 1.0).then_inc(dve_const, 1)
            dve.wait_ge(dve_const, 3 + NG)
            modulation()
            steps(dve, part)

        @block.tensor
        def _(pe):
            def claim(kind, b, tile):
                tiles = TILES[kind]
                n = tiles.index[tile] - (4 if kind in ("start", "end") else 1)
                if n >= 0:
                    on_act, count = tiles.taken(tiles.order[n])
                    before = counts_before(kind, b)
                    pe.wait_ge(tile_act if on_act else tile_dve, after(before[1 if on_act else 2] + count))
                return bank_of(kind, tile)

            def taken(kind, b, tile):
                on_act, count = TILES[kind].taken(tile)
                before = counts_before(kind, b)
                pe.wait_ge(tile_act if on_act else tile_dve, after(before[1 if on_act else 2] + count))

            def values(kind, b, n):
                bank = claim(kind, b, ("v", n))
                for i in range(2):
                    blk = 2 * n + i
                    for k in range(KT):
                        mm = pe.matmul(bank[:, i * D:(i + 1) * D], ht[:, k, blk * P:(blk + 1) * P],
                                       wv[:, k, :], start=(k == 0), stop=(k == KT - 1))
                mm.then_inc(tile_mm, 1)

            def turn(kind, b, batch, t, c):
                bank = claim(kind, b, ("turn", t, c))
                pe.wait_ge(po_evac, after(NC * (NG * batch + t) + c + 1))
                for j in range(CH // P):
                    mm = pe.transpose(bank[:, j * P:(j + 1) * P], ot[:, c, j * P:(j + 1) * P], ident[:, :])
                mm.then_inc(tile_mm, 1)

            def features(kind, b, i):
                bank = claim(kind, b, ("on", i))
                if kind == "end":
                    taken(kind, b, ("turn", NG - 1, NC - 1))
                for k in range(KT):
                    mm = pe.transpose(bank[:, k * P:(k + 1) * P],
                                      on[:, i, 8 * k:8 * k + 8, :].rearrange("p h d -> p (h d)"), ident[:, :])
                mm.then_inc(tile_mm, 1)

            def project_out(kind, b, batch, i):
                bank = claim(kind, b, ("wo", i))
                if kind == "end":
                    taken(kind, b, ("on", i))
                if i == 0:
                    pe.wait_ge(w_scaled, after(6 * batch + 6))
                for k in range(KT):
                    mm = pe.matmul(bank[:, 0:D], ont[:, i % 2, k, :], wo_g[:, k, :],
                                   start=(k == 0), stop=(k == KT - 1))
                mm.then_inc(tile_mm, 1)

            def transpose_h(kind, b, s, batch, i):
                bank = claim(kind, b, ("h", s, i))
                k, ch = i // 2, i % 2
                pe.wait_ge(xn_ready[s], after(NB * batch + 4 * ch + 4))
                for q in range(4):
                    mm = pe.transpose(bank[:, q * P:(q + 1) * P], xn[:, 4 * ch + q, k * P:(k + 1) * P], ident[:, :])
                mm.then_inc(tile_mm, 1)

            def gate_logits(kind, b):
                bank = claim(kind, b, ("gate",))
                if kind == "end":
                    taken(kind, b, ("h", 1, 3))
                for i in range(NB):
                    for k in range(KT):
                        mm = pe.matmul(bank[:, 8 * i:8 * i + E_GATE], ht[:, k, i * P:(i + 1) * P], wg[:, k, :],
                                       start=(k == 0), stop=(k == KT - 1))
                mm.then_inc(tile_mm, 1)

            def ffn(kind, b, i):
                bank = claim(kind, b, ("ffn", i))
                for k in range(KT):
                    mm = pe.matmul(bank, ht[:, k, i * P:(i + 1) * P], wse_g[:, k, :],
                                   start=(k == 0), stop=(k == KT - 1))
                mm.then_inc(tile_mm, 1)

            def project_qk(kind, b, n):
                mt, which, c = n // 4, n // 2 % 2, n % 2
                bank = claim(kind, b, ("qk", n))
                if kind == "start":
                    taken(kind, b, ("h", 0, 3))
                for k in range(KT):
                    mm = pe.matmul(bank, (wq, wk)[which][:, k, mt * P:(mt + 1) * P],
                                   ht[:, k, c * CH:(c + 1) * CH], start=(k == 0), stop=(k == KT - 1))
                mm.then_inc(tile_mm, 1)

            def scores(b, t, k):
                i, half, h0, heads, key0, keys = MAX_TILES[k]
                g = score_group(b, t)
                if k == 0:
                    batch = b + 1 if t == 0 else b
                    pe.wait_ge(stack_loaded[t], after(192 * batch + 192))
                pe.wait_ge(s_red, after(NMT * g + max(k - 1, 0)))
                for h in range(heads):
                    hh = h0 + h
                    o = ps_m[k % 2][:, h * keys:(h + 1) * keys]
                    diagonal = key0 + keys == (i + 1) * P
                    mm = pe.matmul(o, qs[t][0:ROWS, hh, i * P:(i + 1) * P], ks[t][0:ROWS, hh, key0:key0 + keys],
                                   start=True, stop=not diagonal)
                    if diagonal:
                        mm = pe.matmul(o[:, keys - P:keys], ident_b[:, :], mask_b[:, :], start=False, stop=True)
                mm.then_inc(s_mm, 1)

            def transpose_maxima(kind, b, t):
                bank = claim(kind, b, ("m", t))[:, 0:P // 2].bitcast(BF16)
                g = score_group(-1 if kind == "start" else b, t)
                pe.wait_ge(m3_ready, after(g + 1))
                pe.transpose(bank[0:MROWS * HG * NB, :], m3[:, :, :].rearrange("p r n -> p (r n)"),
                             ident_b[:, :]).then_inc(tile_mm, 1)

            def scores_t(kind, b, t, u):
                c, j, first, width, diagonal = UNITS[u]
                if u == 0:
                    pe.wait_ge(mrow_loaded[t], after(48 * b + 48))
                    if kind == "first" and t == 0:
                        taken("start", 0, ("qk", 7))
                        taken("start", 0, ("m", 0))
                for pr in range(2):
                    e = NEXP * t + 2 * u + pr
                    if not (kind == "first" and e < 2):
                        pe.wait_ge(exp_done, after(NEXP * NG * b + e - 1))
                    for h in range(2):
                        hh = 2 * pr + h
                        mm = pe.matmul(ps_t[pr][:, h, 0:width], ks[t][0:ROWS + MROWS, hh, j * P:(j + 1) * P],
                                       qs[t][0:ROWS + MROWS, hh, first:first + width], start=True, stop=True)
                    mm.then_inc(st_mm, 1)

            def weigh_values(kind, b, t, u):
                c, j, first, width, diagonal = UNITS[u]
                last = u + 1 == NU or UNITS[u + 1][0] != c
                pe.wait_ge(exp_done, after(NEXP * (NG * b + t) + 2 * u + 2))
                if diagonal:
                    pe.wait_ge(diag_done, after(NDIAG * (NG * b + t) + sum(x[4] for x in UNITS[:u + 1])))
                if t == 0 and j % 2 == 0:
                    taken(kind, b, ("v", j // 2))
                if j == 0:
                    pe.wait_ge(po_evac, after(NC * (NG * b + t) + c))
                for hh in range(HG):
                    mm = pe.matmul(ps_o[32 * hh:32 * hh + DH + 1, CH - width:CH], v[:, j, HG * t + hh, :],
                                   probs[u % NP_BUF][:, hh, 0:width], start=(j == 0), stop=last)
                mm.then_inc(pv_done, 1)

            def part(kind, b):
                nxt = 0 if kind == "start" else b + 1
                last = b - 1
                for what, *arg in plan_of(kind):
                    if what == "attend":
                        scores_t(kind, b, *arg)
                    elif what == "weigh":
                        weigh_values(kind, b, *arg)
                    elif what == "score":
                        scores(-1 if kind == "start" else b, *arg)
                    elif what == "m":
                        transpose_maxima(kind, b, *arg)
                    elif what == "v":
                        values(kind, b, *arg)
                    elif what == "turn":
                        turn(kind, b, last if tuple(arg) == (NG - 1, NC - 1) else b, *arg)
                    elif what == "on":
                        features(kind, b, *arg)
                    elif what == "wo":
                        project_out(kind, b, last, *arg)
                    elif what == "h":
                        s, i = arg
                        transpose_h(kind, b, s, last if s else nxt, i)
                    elif what == "gate":
                        gate_logits(kind, b)
                    elif what == "ffn":
                        ffn(kind, b, *arg)
                    elif what == "qk":
                        project_qk(kind, b, *arg)

            pe.wait_ge(w_loaded, 16 * N_WLOADS)
            pe.wait_ge(silu_step, 3)
            for m in range(6 * KT):
                for k in range(KT):
                    mm = pe.matmul(ps_x[:, m * B:(m + 1) * B], wm[:, k, m * P:(m + 1) * P], silu[:, k, :],
                                   start=(k == 0), stop=(k == KT - 1))
            mm.then_inc(mod_mm, 1)
            for e, m in enumerate((MOD_GA, MOD_GB)):
                for k in range(KT):
                    mm = pe.matmul(ps_o[0:B, e * D:(e + 1) * D], silu[:, k, :], wm[:, k, m * D:(m + 1) * D],
                                   start=(k == 0), stop=(k == KT - 1))
            mm.then_inc(mod_mm, 1)
            pe.wait_ge(gate_ready, 1)
            pe.wait_ge(pool_const, 9)
            for b in range(B):
                pe.matmul(work[b], sel[:, b, :], grow[:, :], start=True, stop=True).then_inc(bc_mm, 1)
            pe.wait_ge(bc_evac, B + 1)
            steps(pe, part)


def kernel(L0_attn_x, L0_attn_Wq_w, L0_attn_Wq_b, L0_attn_Wk_w, L0_attn_Wk_b, L0_attn_Wv_w, L0_attn_Wv_b,
           L0_attn_Wo_w, L0_attn_Wo_b, L0_ffn_cond, L0_ffn_mask, L0_ffn_W_shared, L0_ffn_W_expert,
           L0_ffn_W_gate, L0_ffn_bias, L0_c, L0_wmod):
    import numpy as np
    import concourse.bacc as bacc
    from concourse.bass_utils import run_bass_kernel_spmd

    def rows(a):
        return np.ascontiguousarray(a)

    def turned(a):
        return np.ascontiguousarray(np.asarray(a).T)

    def line(a):
        return rows(a).reshape(1, -1)

    arrays = {
        "x": rows(L0_attn_x), "wq_t": turned(L0_attn_Wq_w), "wk_t": turned(L0_attn_Wk_w),
        "wv_t": turned(L0_attn_Wv_w), "wo_t": turned(L0_attn_Wo_w), "ws_t": turned(L0_ffn_W_shared),
        "we_t": turned(L0_ffn_W_expert), "wgate": rows(L0_ffn_W_gate),
        "bq": turned(rows(L0_attn_Wq_b).reshape(KT, P)), "bk": turned(rows(L0_attn_Wk_b).reshape(KT, P)),
        "bv": line(L0_attn_Wv_b), "bo": line(L0_attn_Wo_b), "bf": line(L0_ffn_bias),
        "c_t": turned(L0_c), "wmod": rows(L0_wmod),
    }
    nc = bacc.Bacc("TRN2", target_bir_lowering=False, num_devices=1)
    args = {n: nc.dram_tensor(n, a.shape, mybir.dt.from_np(a.dtype), kind="ExternalInput").ap()
            for n, a in arrays.items()}
    args["out"] = nc.dram_tensor("out", (B, T, D), F32, kind="ExternalOutput").ap()
    adaln_block(nc, **args)
    r = run_bass_kernel_spmd(nc, [arrays], core_ids=[0])
    return r.results[0]["out"]
```

```python
from contextlib import ExitStack

import concourse.bass as bass
from concourse import mybir
from concourse.alu_op_type import AluOpType as ALU

ACT = mybir.ActivationFunctionType
AX = mybir.AxisListType
F32 = mybir.dt.float32
BF16 = mybir.dt.bfloat16

P = 128
B, T, D = 4, 1024, 256
H, DH = 16, 16
NB = T // P
KT = D // P
CH = 512
NC = T // CH
HG = 4
NG = H // HG
E_GATE = 7
LN_EPS = 1e-5
GATE_FLOOR = 0.25
SCORE_SCALE = 1.0 / D ** 0.5
MASKED = -3.0e38

Q_PARTS = (0, 0, 1, 1, 0, 2)
K_PARTS = (0, 1, 0, 1, 2, 0)
ROWS = DH * len(Q_PARTS)
MROWS = 3

MOD_SA, MOD_CA, MOD_GA, MOD_SB, MOD_CB, MOD_GB = range(6)


def max_tiles():
    tiles = []
    for i in range(NB):
        for half in range(2):
            keys = min((i + 1) * P - half * CH, CH)
            if keys <= 0:
                continue
            heads = max(n for n in (1, 2, 4) if n * keys <= CH)
            for h in range(0, HG, heads):
                tiles.append((i, half, h, heads, half * CH, keys))
    return tiles


def units():
    out = []
    for c in range(NC):
        for j in range((c + 1) * CH // P):
            first = max(c * CH, j * P)
            out.append((c, j, first, (c + 1) * CH - first, j * P >= c * CH))
    return out


MAX_TILES = max_tiles()
UNITS = units()
NMT, NU = len(MAX_TILES), len(UNITS)
NEXP = 2 * NU
NDIAG = sum(u[4] for u in UNITS)
NP_BUF = 3
CHUNK_END = [sum(u[0] <= c for u in UNITS) for c in range(NC)]
NSU = NG * NU

ON_ACT = ("on", "h", "qk", "bc")


def tiles_of_batch():
    at = [(n if n < 2 else 2 * n, ("v", n)) for n in range(NB // 2)]
    for t in range(NG):
        for c in range(NC):
            if (t, c) != (NG - 1, NC - 1):
                at.append((NU * t + CHUNK_END[c] + 2, ("turn", t, c)))
    at += [(WINDOWS[t][1] + 1, ("m", t)) for t in range(1, NG)]
    return at


def tiles_of_last():
    at = [(0, ("turn", NG - 1, NC - 1))]
    at += [(1 + i, ("on", i)) for i in range(NB)]
    at += [(2 + i, ("wo", i)) for i in range(NB)]
    at += [(12 + i // 2, ("h", 1, i)) for i in range(4)]
    at += [(14, ("gate",))]
    at += [(18 + i // 2, ("ffn", i)) for i in range(NB)]
    return at


def tiles_of_next():
    at = [(22 + i // 2, ("h", 0, i)) for i in range(4)]
    at += [(24 + n + 6 * (n // 4), ("qk", n)) for n in range(8)]
    at += [(WINDOWS[0][1] + 1, ("m", 0))]
    return at


def local_of_last():
    at = [(10, ("aggregate", 1))] + [(11, ("normalise", 1, i)) for i in range(2)]
    at += [(13 + i // 2, ("bias", 1, i)) for i in range(NB)]
    at += [(15, ("gate_soft",)), (16, ("gate_top", 0)), (16, ("gate_top", 1)), (17, ("gate_top", 2)),
           (17, ("gate_top", 3))]
    return at


def local_of_next():
    at = [(12 + i // 2, ("stats", i)) for i in range(NB)]
    at += [(18, ("aggregate", 0))] + [(20 + i, ("normalise", 0, i)) for i in range(2)]
    at += [(25 + n + 6 * (n // 4), ("rest", n)) for n in range(8)]
    at += [(26 + n + 6 * (n // 4), ("second_part", n)) for n in range(8)]
    return at


WINDOWS = {1: (0, 9), 2: (9, 20), 3: (20, 32), 0: (35, NSU - 3)}


def max_tiles_by_unit(last):
    by_unit = [[] for _ in range(NSU)]
    for t, (u0, u1) in WINDOWS.items():
        if t == 0 and last:
            continue
        cost = [x[3] * x[5] for x in MAX_TILES]
        widths = [UNITS[u % NU][3] for u in range(u0, u1)]
        done = k = 0
        for u in range(u0, u1):
            share = sum(cost) * sum(widths[:u + 1 - u0]) / sum(widths)
            while k < NMT and done < share - 1e-9:
                done += cost[k]
                by_unit[u].append(("score", t, k))
                k += 1
        assert k == NMT
    return by_unit


def merged(*lists):
    placed = [((k + 0.5) / len(x), n, item) for n, x in enumerate(lists) for k, item in enumerate(x)]
    return [(at, item) for at, n, item in sorted(placed, key=lambda y: y[:2])]


def step_plan(kind):
    tiles = tiles_of_batch()
    local = [((29, 30, 37, 38)[i], ("scale", i)) for i in range(4)] + [(40 + i // 2, ("bias", 0, i)) for i in range(NB)]
    if kind != "first":
        tiles += tiles_of_last()
        local += local_of_last()
    if kind != "last":
        tiles += tiles_of_next()
        local += local_of_next()
    scores = max_tiles_by_unit(kind == "last")
    plan = []
    for u in range(NSU):
        beside = merged(*([x for at, x in sorted(of, key=lambda y: y[0]) if at == u] for of in (tiles, local)),
                        scores[u])
        own = [(0, ("attend", u // NU, u % NU, 0)), (0.35, ("attend", u // NU, u % NU, 1))]
        if u:
            own.append((0.7, ("weigh", (u - 1) // NU, (u - 1) % NU)))
        plan += [x for at, x in sorted(own + beside, key=lambda y: y[0])]
        plan += [("split_max", t) for t, w in WINDOWS.items() if ("score", t, NMT - 1) in scores[u]]
    plan.append(("weigh", NG - 1, NU - 1))
    return plan


def start_plan():
    plan = [("stats", i) for i in range(NB)] + [("aggregate", 0), ("normalise", 0, 0), ("normalise", 0, 1)]
    plan += [("h", 0, i) for i in range(4)] + [("modulation",)]
    for n in range(10):
        plan += [("bc", i) for i in range(B)] if n == 4 else []
        plan += [("qk", n)] if n < 8 else []
        plan += [("second_part", n - 2)] if n >= 2 else []
        plan += [("rest", n - 1)] if 1 <= n <= 8 else []
    return plan + [("score", 0, k) for k in range(NMT)] + [("split_max", 0), ("m", 0)]


def end_plan():
    plan = [("turn", NG - 1, NC - 1)]
    for i in range(NB + 1):
        plan += [("on", i)] if i < NB else []
        plan += [("wo", i - 1)] if i else []
    plan += [("aggregate", 1), ("normalise", 1, 0), ("normalise", 1, 1)] + [("bias", 1, i) for i in range(NB)]
    plan += [("h", 1, i) for i in range(4)]
    return plan + [("gate",), ("gate_soft",)] + [("gate_top", i) for i in range(4)] + [("ffn", i) for i in range(NB)]


TILE_KINDS = ("v", "turn", "on", "wo", "h", "gate", "ffn", "qk", "m", "bc", "score")


class Tiles:

    def __init__(self, plan):
        self.order = [x for x in plan if x[0] in TILE_KINDS]
        self.index = {x: n for n, x in enumerate(self.order)}
        self.all, self.act = len(self.order), sum(x[0] in ON_ACT for x in self.order)
        self.dve = self.all - self.act

    def taken(self, tile):
        upto = self.order[:self.index[tile] + 1]
        on_act = tile[0] in ON_ACT
        return on_act, sum((x[0] in ON_ACT) == on_act for x in upto)


START, END = start_plan(), end_plan()
STEPS = {kind: step_plan(kind) for kind in ("first", "middle", "last")}
TILES = {"start": Tiles(START), "end": Tiles(END), **{k: Tiles(p) for k, p in STEPS.items()}}


def counts_before(kind, b):
    start, first, middle, last = (TILES[k] for k in ("start", "first", "middle", "last"))

    def count(what):
        n = {"start": 0, "first": what(start)}
        n["middle"] = (b - 1) * what(middle) + what(start) + what(first)
        n["last"] = (B - 2) * what(middle) + what(start) + what(first)
        n["end"] = n["last"] + what(last)
        return n[kind]

    if kind != "middle":
        b = 1
    return count(lambda t: t.all), count(lambda t: t.act), count(lambda t: t.dve)


def adaln_block(nc, x, wq_t, wk_t, wv_t, wo_t, ws_t, we_t, wgate, bq, bk, bv, bo, bf, c_t, wmod, out):
    with ExitStack() as ctx:
        def sb(name, shape, dt=F32):
            return ctx.enter_context(nc.sbuf_tensor(name, shape, dt))

        def pb(name, shape, dt=F32):
            return ctx.enter_context(nc.psum_tensor(name, shape, dt))

        def sem(name):
            return ctx.enter_context(nc.semaphore(name))

        counted = []

        def counted_sem(name):
            counted.append(sem(name))
            return counted[-1]

        def after(n):
            return n + 1

        wq = sb("wq", [P, KT, D])
        wk = sb("wk", [P, KT, D])
        wv = sb("wv", [P, KT, D])
        wo = sb("wo", [P, KT, D])
        wse = sb("wse", [P, KT, 2 * D])
        wg = sb("wg", [P, KT, E_GATE])
        wo_g = sb("wo_g", [P, KT, D])
        wse_g = sb("wse_g", [P, KT, 2 * D])
        bqk = sb("bqk", [P, 2, KT])
        bv_bc = sb("bv_bc", [P, D])
        bob_bc = sb("bob_bc", [P, 2, D])
        gate_bc = sb("gate_bc", [P, B, 2, D])
        gbias = sb("gbias", [P, 2, D])
        modc = sb("modc", [P, 6, KT, B])
        ct = sb("ct", [P, KT, B])
        ect = sb("ect", [P, KT, B])
        silu = sb("silu", [P, KT, B])
        grow = sb("grow", [B, 2 * D])
        sel = sb("sel", [B, B, P])
        ident = sb("ident", [P, P])
        ident_b = sb("ident_b", [P, P], BF16)
        mask_b = sb("mask_b", [P, P], BF16)
        nhalf = sb("nhalf", [P, NB])
        xs = sb("xs", [P, NB, D])
        xn = sb("xn", [P, NB, D])
        ht = sb("ht", [P, KT, T])
        stats = sb("stats", [P, NB, 6])
        mv = sb("mv", [P, NB, 2])
        ve = sb("ve", [P, NB])
        rstd = sb("rstd", [P, NB])
        stage = sb("stage", [P, 2, CH])
        rest = sb("rest", [P, 2, CH])
        parts = sb("parts", [P, 2, 3, T], BF16)
        wm = parts[:, :, :, :].rearrange("p w r n -> p (w r n)").bitcast(F32).rearrange("p (k n) -> p k n", k=KT)
        v = sb("v", [P, NB, H, DH + 1])
        qs = [sb(f"qs{t}", [ROWS + MROWS, HG, T], BF16) for t in range(NG)]
        ks = [sb(f"ks{t}", [ROWS + MROWS, HG, T], BF16) for t in range(NG)]
        mpart = sb("mpart", [P, HG, NB, 2])
        mx = sb("mx", [P, HG * NB])
        mrest = sb("mrest", [P, HG * NB])
        m3 = sb("m3", [P, MROWS, HG * NB], BF16)
        mrow = sb("mrow", [MROWS * HG * NB, P], BF16)
        probs = [sb(f"probs{i}", [P, HG, CH]) for i in range(NP_BUF)]
        gsign, gabs = probs[0][0:B, 0, :], probs[0][0:B, 1, :]
        ot = sb("ot", [P, 2, CH])
        rec = sb("rec", [P, NC, CH // P, HG])
        on = sb("on", [P, NB, H, DH])
        ont = sb("ont", [P, 2, KT, P])
        x1 = sb("x1", [P, NB, D])
        logit = sb("logit", [P, NB, 8])
        lmax = sb("lmax", [P, NB])
        lexp = sb("lexp", [P, NB, 8])
        lsum = sb("lsum", [P, NB])
        score = sb("score", [P, NB, 8])
        top8 = sb("top8", [P, NB, 8])
        tsum = sb("tsum", [P, NB])
        wtop = sb("wtop", [P, NB, 2])
        wsum = sb("wsum", [P, NB])
        y = sb("y", [P, 2, D])

        ps_t = [pb(f"ps_t{i}", [P, 2, CH]) for i in range(2)]
        work = [ps_t[i // 2][:, i % 2, :] for i in range(4)]
        ps_o = pb("ps_o", [P, CH])
        ps_x = [pb(f"ps_x{i}", [P, CH]) for i in range(3)]
        scratch = nc.dram_tensor("parts_scratch", [B, 2, 3, D, T], BF16, kind="Internal").ap()

        w_loaded = sem("w_loaded")
        c_loaded = sem("c_loaded")
        wm_loaded = sem("wm_loaded")
        x_loaded = counted_sem("x_loaded")
        pool_const = sem("pool_const")
        dve_const = sem("dve_const")
        c_exp = sem("c_exp")
        silu_step = sem("silu_step")
        mod_mm = sem("mod_mm")
        mod_step = sem("mod_step")
        gate_ready = sem("gate_ready")
        gbias_ready = counted_sem("gbias_ready")
        w_scaled = counted_sem("w_scaled")
        x1_loaded = counted_sem("x1_loaded")
        tile_mm = counted_sem("tile_mm")
        tile_act = counted_sem("tile_act")
        tile_dve = counted_sem("tile_dve")
        ln_stats = [counted_sem(f"ln{s}_stats") for s in range(2)]
        ln_mv = [counted_sem(f"ln{s}_mv") for s in range(2)]
        ln_rstd = [counted_sem(f"ln{s}_rstd") for s in range(2)]
        xn_ready = [counted_sem(f"xn{s}_ready") for s in range(2)]
        p1_ready = counted_sem("p1_ready")
        r_ready = counted_sem("r_ready")
        p2_ready = counted_sem("p2_ready")
        p3_ready = counted_sem("p3_ready")
        parts_stored = [counted_sem(f"parts_stored{i}") for i in range(KT)]
        stack_loaded = [counted_sem(f"stack_loaded{t}") for t in range(NG)]
        mrow_loaded = [counted_sem(f"mrow_loaded{t}") for t in range(NG)]
        m_step = counted_sem("m_step")
        m3_ready = counted_sem("m3_ready")
        st_mm = counted_sem("st_mm")
        exp_done = counted_sem("exp_done")
        diag_done = counted_sem("diag_done")
        pv_done = counted_sem("pv_done")
        po_evac = counted_sem("po_evac")
        rec_ready = counted_sem("rec_ready")
        x1_biased = counted_sem("x1_biased")
        x1b_ready = counted_sem("x1b_ready")
        g_step = counted_sem("g_step")
        g_exp = counted_sem("g_exp")
        y_ready = counted_sem("y_ready")
        out_stored = counted_sem("out_stored")

        N_WLOADS = 12
        G_STEPS = 6 + NB + 4

        xv = x.rearrange("b (n p) d -> b p n d", p=P)
        ov = out.rearrange("b (n p) d -> b p n d", p=P)

        def apart(engine):
            engine.nop(nofuse=True)

        def tile_wait(engine, kind, b, tile):
            engine.wait_ge(tile_mm, after(counts_before(kind, b)[0] + TILES[kind].index[tile] + 1))

        def bank_of(kind, tile):
            n = TILES[kind].index[tile]
            return work[n % 4] if kind in ("start", "end") else ps_x[n % 3][:, :]

        def score_group(b, t):
            return NG * (b + 1) if t == 0 else NG * b + t

        def steps(engine, part):
            part("start", 0)
            part("first", 0)
            with engine.Fori(1, B - 1) as b:
                part("middle", b)
            part("last", B - 1)
            part("end", B)

        def plan_of(kind):
            return {"start": START, "end": END}.get(kind) or STEPS[kind]

        block = ctx.enter_context(nc.Block())

        @block.sync
        def _(sp):
            def at_batch(b):
                return bass.ds(b, 1)

            def load_x(b, dst, loaded):
                sp.dma_start(dst[:, :, :], xv[at_batch(b)].rearrange("o p n d -> (o p) n d")).then_inc(loaded, 16)

            def store_parts(b, mt):
                for which in range(2):
                    sp.wait_ge(p3_ready, after(8 * b + 4 * mt + 2 * which + 2))
                    for part in range(3):
                        sp.dma_start(scratch[at_batch(b), which, part, mt * P:(mt + 1) * P, :]
                                     .rearrange("o p n -> (o p) n"),
                                     parts[:, which, part, :]).then_inc(parts_stored[mt], 16)

            def load_stacks(b, t, later):
                sp.wait_ge(parts_stored[t // 2], after(96 * b + 96))
                if later:
                    apart(sp)
                    sp.wait_ge(st_mm, after(NEXP * (NG * (b - 1) + t + 1)))
                f0 = t * HG * DH
                for which, dst, order in ((0, qs, Q_PARTS), (1, ks, K_PARTS)):
                    for r, part in enumerate(order):
                        src = scratch[at_batch(b), which, part, f0:f0 + HG * DH, :]
                        sp.dma_start(dst[t][r * DH:(r + 1) * DH, :, :],
                                     src.rearrange("o (h d) n -> (o d) h n", d=DH)
                                     ).then_inc(stack_loaded[t], 16)

            def taken(kind, b, tile):
                sp.wait_ge(tile_dve, after(counts_before(kind, b)[2] + TILES[kind].taken(tile)[1]))

            def load_rows(kind, b, batch, t):
                taken(kind, b, ("m", t))
                n = HG * NB
                for r in range(MROWS):
                    sp.dma_start(qs[t][ROWS + r:ROWS + r + 1, :, :].rearrange("o h (i q) -> o (h i) q", q=P),
                                 mrow[r * n:(r + 1) * n, :]).then_inc(mrow_loaded[t], 16)

            def store_out(kind, b, batch, half):
                n0 = half * NB // 2
                taken(kind, b, ("ffn", n0 + NB // 2 - 1))
                sp.dma_start(ov[at_batch(batch), :, n0:n0 + NB // 2, :].rearrange("o p n d -> (o p) n d"),
                             x1[:, n0:n0 + NB // 2, :]).then_inc(out_stored, 16)

            def part(kind, b):
                if kind == "start":
                    store_parts(0, 0)
                    load_stacks(0, 0, False)
                    store_parts(0, 1)
                    load_stacks(0, 1, False)
                    load_stacks(0, 2, False)
                    load_rows("start", 0, 0, 0)
                    return
                if kind == "end":
                    store_out("end", B, B - 1, 0)
                    store_out("end", B, B - 1, 1)
                    return
                last, this, next_ = b - 1, b, b + 1
                if kind == "middle":
                    last, next_ = sp.snap(b - 1), sp.snap(b + 1)
                load_stacks(this, 3, kind != "first")
                if kind != "last":
                    sp.wait_ge(xn_ready[0], after(NB * this + NB))
                    load_x(next_, xs, x_loaded)
                load_rows(kind, b, this, 1)
                if kind != "first":
                    store_out(kind, b, last, 0)
                load_rows(kind, b, this, 2)
                if kind != "first":
                    store_out(kind, b, last, 1)
                    sp.wait_ge(out_stored, after(32 * this))
                    load_x(this, x1, x1_loaded)
                else:
                    load_x(this, x1, x1_loaded)
                if kind != "last":
                    store_parts(next_, 0)
                    load_stacks(next_, 0, True)
                load_rows(kind, b, this, 3)
                if kind != "last":
                    load_stacks(next_, 1, True)
                    store_parts(next_, 1)
                    load_stacks(next_, 2, True)
                    load_rows(kind, b, next_, 0)

            sp.dma_start(xs[:, :, :], xv[0]).then_inc(x_loaded, 16)
            for s in counted:
                sp.sem_inc(s, 1)
            sp.dma_start(ct[:, :, :], c_t.rearrange("(k p) n -> p k n", p=P)).then_inc(c_loaded, 16)
            sp.dma_start(wm[:, :, :], wmod.rearrange("(k p) n -> p k n", p=P)).then_inc(wm_loaded, 16)
            sp.dma_start(bqk[:, 0, :], bq).then_inc(w_loaded, 16)
            sp.dma_start(bqk[:, 1, :], bk).then_inc(w_loaded, 16)
            for dst, src in ((wq, wq_t), (wk, wk_t), (wv, wv_t), (wo, wo_t)):
                sp.dma_start(dst[:, :, :], src.rearrange("(k p) n -> p k n", p=P)).then_inc(w_loaded, 16)
            sp.dma_start(wse[:, :, 0:D], ws_t.rearrange("(k p) n -> p k n", p=P)).then_inc(w_loaded, 16)
            sp.dma_start(wse[:, :, D:2 * D], we_t.rearrange("(k p) n -> p k n", p=P)).then_inc(w_loaded, 16)
            sp.dma_start(wg[:, :, :], wgate.rearrange("(k p) n -> p k n", p=P)).then_inc(w_loaded, 16)
            for dst, src in ((bv_bc[:, :], bv), (bob_bc[:, 0, :], bo), (bob_bc[:, 1, :], bf)):
                sp.dma_start(dst, src.to_broadcast([P, D])).then_inc(w_loaded, 16)
            steps(sp, part)
            sp.wait_ge(out_stored, after(2 * 16 * B))
            for mt in range(KT):
                sp.wait_ge(parts_stored[mt], after(96 * B))

        @block.gpsimd
        def _(pool):
            def consts():
                pool.memset(ident[:, :], 0.0).then_inc(pool_const, 1)
                pool.memset(ident_b[:, :], 0.0).then_inc(pool_const, 1)
                pool.memset(mask_b[:, :], 0.0).then_inc(pool_const, 1)
                pool.memset(sel[:, :, :], 0.0).then_inc(pool_const, 1)
                pool.memset(nhalf[:, :], -0.5).then_inc(pool_const, 1)
                pool.wait_ge(pool_const, 5)
                for m in (ident, ident_b):
                    pool.affine_select(out=m[:, :], in_=m[:, :], compare_op=ALU.not_equal, fill=1.0, base=0,
                                       pattern=[[-1, P]], channel_multiplier=1).then_inc(pool_const, 1)
                pool.affine_select(out=mask_b[:, :], in_=mask_b[:, :], compare_op=ALU.is_ge, fill=MASKED,
                                   base=0, pattern=[[-1, P]], channel_multiplier=1).then_inc(pool_const, 1)
                pool.affine_select(out=sel[:, :, :], in_=sel[:, :, :], compare_op=ALU.not_equal, fill=1.0,
                                   base=0, pattern=[[-1, B], [0, P]], channel_multiplier=1).then_inc(pool_const, 1)
                for n, t in enumerate((2, 3)):
                    pool.wait_ge(pool_const, 9 + n)
                    pool.memset(ks[t][ROWS:ROWS + MROWS, :, :], 1.0).then_inc(pool_const, 1)

            def scale_weights(kind, b, piece):
                ga = gate_bc[:, bass.ds(b, 1), 0, :]
                gb = gate_bc[:, bass.ds(b, 1), 1, :]
                if piece == 0:
                    if kind == "first":
                        pool.wait_ge(w_loaded, 16 * N_WLOADS)
                        pool.wait_ge(tile_act, after(TILES["start"].taken(("bc", B - 1))[1]))
                    else:
                        pool.wait_ge(tile_dve, after(counts_before(kind, b)[2] + TILES[kind].taken(("ffn", NB - 1))[1]))
                        pool.wait_ge(x1b_ready, after(NB * b))
                        apart(pool)
                    for e, g in enumerate((ga, gb)):
                        pool.tensor_tensor(gbias[:, e:e + 1, :], bob_bc[:, e:e + 1, :], g,
                                           ALU.mult).then_inc(gbias_ready, 1)
                elif piece == 1:
                    for k in range(KT):
                        pool.tensor_tensor(wo_g[:, k:k + 1, :], wo[:, k:k + 1, :], ga, ALU.mult).then_inc(w_scaled, 1)
                else:
                    k = piece - 2
                    for e in range(2):
                        pool.tensor_tensor(wse_g[:, k:k + 1, e * D:(e + 1) * D], wse[:, k:k + 1, e * D:(e + 1) * D],
                                           gb, ALU.mult).then_inc(w_scaled, 1)

            def rstd_of(s, b):
                pool.wait_ge(ln_mv[s], after(NB * b + NB))
                apart(pool)
                pool.tensor_scalar(ve[:, :], mv[:, :, 1], LN_EPS, None, ALU.add).then_inc(ln_rstd[s], 1)
                pool.wait_ge(ln_rstd[s], after(2 * b + 1))
                pool.tensor_tensor(rstd[:, :], ve[:, :], nhalf[:, :], ALU.pow).then_inc(ln_rstd[s], 1)

            def add_bias(b, which, i):
                if which == 0 and i == 0:
                    pool.wait_ge(x1_loaded, after(16 * b + 16))
                    pool.wait_ge(gbias_ready, after(2 * b + 2))
                elif which == 1 and i == 0:
                    pool.wait_ge(xn_ready[1], after(NB * b + NB))
                pool.tensor_tensor(x1[:, i, :], x1[:, i, :], gbias[:, which, :],
                                   ALU.add).then_inc(x1b_ready if which else x1_biased, 1)

            def rest_of(kind, step, b, n):
                mt, which, c = n // 4, n // 2 % 2, n % 2
                pool.wait_ge(p1_ready, after(8 * b + n + 1))
                pool.wait_ge(tile_act, after(counts_before(kind, step)[1] + TILES[kind].taken(("qk", n))[1]))
                pool.wait_ge(p3_ready, after(8 * b + max(n - 1, 0)))
                pool.tensor_tensor(rest[:, n % 2, :], stage[:, n % 2, :],
                                   parts[:, which, 0, c * CH:(c + 1) * CH], ALU.subtract).then_inc(r_ready, 1)

            def third_part(b, n):
                mt, which, c = n // 4, n // 2 % 2, n % 2
                pool.wait_ge(p2_ready, after(8 * b + n + 1))
                pool.tensor_tensor(parts[:, which, 2, c * CH:(c + 1) * CH], rest[:, n % 2, :],
                                   parts[:, which, 1, c * CH:(c + 1) * CH], ALU.subtract).then_inc(p3_ready, 1)

            def mask_diagonal(b, t, u):
                pool.wait_ge(exp_done, after(NEXP * (NG * b + t) + 2 * u + 2))
                pr = probs[u % NP_BUF][:, :, 0:P]
                apart(pool)
                pool.affine_select(out=pr, in_=pr, compare_op=ALU.is_ge, fill=0.0, base=0,
                                   pattern=[[0, HG], [1, P]], channel_multiplier=-1).then_inc(diag_done, 1)

            def part(kind, b):
                nxt = 0 if kind == "start" else b + 1
                for what, *arg in plan_of(kind):
                    if what == "attend" and UNITS[arg[1]][4] and arg[2] == 1:
                        mask_diagonal(b, *arg[:2])
                    elif what == "aggregate":
                        s, = arg
                        rstd_of(s, b - 1 if s else nxt)
                    elif what == "scale":
                        scale_weights(kind, b, *arg)
                    elif what == "bias":
                        which, i = arg
                        add_bias(b - 1 if which else b, which, i)
                    elif what == "rest":
                        rest_of(kind, b, nxt, *arg)
                    elif what == "second_part":
                        third_part(nxt, *arg)

            consts()
            pool.wait_ge(pool_const, 11)
            steps(pool, part)

        @block.scalar
        def _(act):
            def modulate(kind, b, batch, s, i):
                shift, scale = (MOD_SB, MOD_CB) if s else (MOD_SA, MOD_CA)
                k, ch = i // 2, i % 2
                tile_wait(act, kind, b, ("h", s, i))
                apart(act)
                act.activation(ht[:, k, ch * CH:(ch + 1) * CH], bank_of(kind, ("h", s, i)), ACT.Identity,
                               bias=modc[:, shift, k, bass.ds(batch, 1)],
                               scale=modc[:, scale, k, bass.ds(batch, 1)]).then_inc(tile_act, 1)

            def stage_qk(kind, b, batch, n):
                mt, which, c = n // 4, n // 2 % 2, n % 2
                if n == 4:
                    act.wait_ge(parts_stored[0], after(96 * batch + 96))
                elif n == 0 and kind != "start":
                    act.wait_ge(parts_stored[1], after(96 * batch))
                elif n == 0:
                    act.wait_ge(w_loaded, 16 * N_WLOADS)
                tile_wait(act, kind, b, ("qk", n))
                bank = bank_of(kind, ("qk", n))
                act.activation(parts[:, which, 0, c * CH:(c + 1) * CH], bank, ACT.Identity,
                               bias=bqk[:, which, mt:mt + 1]).then_inc(p1_ready, 1)
                act.wait_ge(r_ready, after(8 * batch + max(n - 1, 0)))
                act.activation(stage[:, n % 2, :], bank, ACT.Identity,
                               bias=bqk[:, which, mt:mt + 1]).then_inc(tile_act, 1)

            def chunk_out(b, t, c):
                act.wait_ge(pv_done, after(NU * (NG * b + t) + CHUNK_END[c]))
                act.activation(ot[:, c, :], ps_o[:, :], ACT.Copy).then_inc(po_evac, 1)

            def exps(kind, b, t, u, pr):
                width = UNITS[u][3]
                if pr == 0 and not (kind == "first" and NU * t + u < NP_BUF):
                    act.wait_ge(pv_done, after(NSU * b + NU * t + u - NP_BUF + 1))
                act.wait_ge(st_mm, after(NEXP * (NG * b + t) + 2 * u + pr + 1))
                act.activation(probs[u % NP_BUF][:, 2 * pr:2 * pr + 2, 0:width], ps_t[pr][:, :, 0:width],
                               ACT.Exp, scale=SCORE_SCALE).then_inc(exp_done, 1)

            def part(kind, b):
                nxt = 0 if kind == "start" else b + 1
                for what, *arg in plan_of(kind):
                    if what == "attend":
                        exps(kind, b, *arg)
                    elif what == "weigh":
                        t, u = arg
                        for c in range(NC):
                            if u + 1 == CHUNK_END[c]:
                                chunk_out(b, t, c)
                    elif what == "bc":
                        tile_wait(act, kind, b, (what, *arg))
                        act.activation(gate_bc[:, arg[0], :, :].rearrange("p a d -> p (a d)"),
                                       bank_of(kind, (what, *arg)), ACT.Copy).then_inc(tile_act, 1)
                    elif what == "h":
                        s, i = arg
                        if kind == "start" and i == 0:
                            act.wait_ge(mod_step, 3)
                        modulate(kind, b, b - 1 if s else nxt, s, i)
                    elif what == "qk":
                        stage_qk(kind, b, nxt, *arg)
                    elif what == "on":
                        i, = arg
                        tile_wait(act, kind, b, ("on", i))
                        act.activation(ont[:, i % 2, :, :],
                                       bank_of(kind, ("on", i))[:, 0:D].rearrange("p (k n) -> p k n", k=KT),
                                       ACT.Copy).then_inc(tile_act, 1)
                    elif what == "gate_soft":
                        act.wait_ge(g_step, after(G_STEPS * (b - 1) + 3))
                        act.activation(lexp[:, :, :], lexp[:, :, :], ACT.Exp).then_inc(g_exp, 1)

            act.wait_ge(c_loaded, 16)
            act.activation(ect[:, :, :], ct[:, :, :], ACT.Exp, scale=-1.0).then_inc(c_exp, 1)
            steps(act, part)

        @block.vector
        def _(dve):
            def spread(a, n):
                return a[:, :].rearrange("p (i o) -> p i o", o=1).to_broadcast([P, NB, n])

            def statistics(s, src, i):
                dve.bn_stats(stats[:, i, :], src[:, i, :]).then_inc(ln_stats[s], 1)

            def aggregate(s, batch):
                for i in range(NB):
                    dve.wait_ge(ln_stats[s], after(NB * batch + i + 1))
                    apart(dve)
                    dve.bn_aggr(mv[:, i, :], stats[:, i, :]).then_inc(ln_mv[s], 1)

            def normalise(kind, b, s, half, batch, src):
                dve.wait_ge(ln_rstd[s], after(2 * batch + 2))
                before = counts_before(kind, b)[0]
                if kind in ("middle", "last") and s == 0:
                    before = before + TILES[kind].index[("h", 1, 3)] + 1
                if kind != "start":
                    dve.wait_ge(tile_mm, after(before))
                for i in range(half * NB // 2, (half + 1) * NB // 2):
                    dve.tensor_scalar(xn[:, i, :], src[:, i, :], mv[:, i, 0:1], rstd[:, i:i + 1],
                                      ALU.subtract, ALU.mult).then_inc(xn_ready[s], 1)

            def second_part(batch, n):
                mt, which, c = n // 4, n // 2 % 2, n % 2
                dve.wait_ge(r_ready, after(8 * batch + n + 1))
                dve.tensor_copy(parts[:, which, 1, c * CH:(c + 1) * CH],
                                rest[:, n % 2, :]).then_inc(p2_ready, 1)

            def values(kind, b, n):
                tile_wait(dve, kind, b, ("v", n))
                for i in range(2):
                    ins = dve.tensor_tensor(v[:, 2 * n + i, :, 0:DH],
                                            bank_of(kind, ("v", n))[:, i * D:(i + 1) * D]
                                            .rearrange("p (h d) -> p h d", d=DH),
                                            bv_bc[:, :].rearrange("p (h d) -> p h d", d=DH), ALU.add)
                ins.then_inc(tile_dve, 1)

            def maximum(kind, b, t, k):
                i, half, h0, heads, key0, keys = MAX_TILES[k]
                tile_wait(dve, kind, b, ("score", t, k))
                dve.tensor_reduce(mpart[:, h0:h0 + heads, i, half],
                                  bank_of(kind, ("score", t, k))[:, 0:heads * keys]
                                  .rearrange("p (h n) -> p h n", h=heads),
                                  AX.X, ALU.max).then_inc(tile_dve, 1)

            def split_maxima(kind, b, t):
                g = score_group(-1 if kind == "start" else b, t)
                dve.wait_ge(tile_dve, after(counts_before(kind, b)[2] + TILES[kind].taken(("score", t, NMT - 1))[1]))
                dve.tensor_reduce(mx[:, :], mpart[:, :, :, :].rearrange("p h i a -> p (h i) a"),
                                  AX.X, ALU.max).then_inc(m_step, 1)
                dve.wait_ge(m_step, after(4 * g + 1))
                dve.tensor_scalar(m3[:, 0, :], mx[:, :], -1.0, None, ALU.mult).then_inc(m_step, 1)
                dve.wait_ge(m_step, after(4 * g + 2))
                dve.scalar_tensor_tensor(out=mrest[:, :], in0=mx[:, :], scalar=-1.0, in1=m3[:, 0, :],
                                         op0=ALU.mult, op1=ALU.subtract).then_inc(m_step, 1)
                dve.wait_ge(m_step, after(4 * g + 3))
                dve.tensor_copy(m3[:, 1, :], mrest[:, :]).then_inc(m_step, 1)
                dve.wait_ge(m_step, after(4 * g + 4))
                dve.tensor_tensor(m3[:, 2, :], mrest[:, :], m3[:, 1, :], ALU.subtract).then_inc(m3_ready, 1)

            def maxima_rows(kind, b, t):
                tile_wait(dve, kind, b, ("m", t))
                if kind != "start":
                    dve.wait_ge(mrow_loaded[(t - 1) % NG], after(48 * b + 48))
                bank = bank_of(kind, ("m", t))[:, 0:P // 2].bitcast(BF16)
                dve.tensor_copy(mrow[:, :], bank[0:MROWS * HG * NB, :]).then_inc(tile_dve, 1)

            def turn(kind, b, batch, t, c):
                tile_wait(dve, kind, b, ("turn", t, c))
                bank = bank_of(kind, ("turn", t, c))
                dve.reciprocal(rec[:, c, :, :].rearrange("p k h -> p (k h)"),
                               bank.rearrange("p (n r) -> p n r", r=2 * DH)[:, :, DH]).then_inc(rec_ready, 1)
                dve.wait_ge(rec_ready, after(NC * (NG * batch + t) + c + 1))
                k = CH // P
                for j in range(k):
                    ins = dve.tensor_tensor(on[:, k * c + j, HG * t:HG * t + HG, :],
                                            bank[:, j * P:(j + 1) * P].rearrange("p (h r) -> p h r", h=HG)[:, :, 0:DH],
                                            rec[:, c, j, :].rearrange("p (h o) -> p h o", o=1).to_broadcast([P, HG, DH]),
                                            ALU.mult)
                ins.then_inc(tile_dve, 1)

            def output(kind, b, batch, i):
                tile_wait(dve, kind, b, ("wo", i))
                if i == 0:
                    dve.wait_ge(x1_biased, after(NB * batch + NB))
                dve.tensor_tensor(x1[:, i, :], bank_of(kind, ("wo", i))[:, 0:D], x1[:, i, :],
                                  ALU.add).then_inc(tile_dve, 1)
                dve.wait_ge(tile_dve, after(counts_before(kind, b)[2] + TILES[kind].taken(("wo", i))[1]))
                statistics(1, x1, i)

            def linker(batch, done):
                step = [done]

                def link(ins):
                    step[0] += 1
                    ins.then_inc(g_step, 1)
                    dve.wait_ge(g_step, after(G_STEPS * batch + step[0]))

                return link

            def take_logits(kind, b):
                tile_wait(dve, kind, b, ("gate",))
                dve.tensor_copy(logit[:, :, 0:E_GATE],
                                bank_of(kind, ("gate",))[:, 0:8 * NB]
                                .rearrange("p (i e) -> p i e", e=8)[:, :, 0:E_GATE]).then_inc(tile_dve, 1)

            def gate_softmax(kind, b, batch):
                link = linker(batch, 0)
                dve.wait_ge(tile_dve, after(counts_before(kind, b)[2] + TILES[kind].taken(("gate",))[1]))
                link(dve.tensor_reduce(lmax[:, :], logit[:, :, :], AX.X, ALU.max))
                dve.tensor_tensor(lexp[:, :, :], logit[:, :, :], spread(lmax, 8), ALU.subtract).then_inc(g_step, 2)

            def gate_top(batch, piece):
                link = linker(batch, (3, 6, 6 + NB // 2, 6 + NB)[piece])
                if piece == 0:
                    dve.wait_ge(g_exp, after(batch + 1))
                    link(dve.tensor_reduce(lsum[:, :], lexp[:, :, :], AX.X, ALU.add))
                    link(dve.reciprocal(lsum[:, :], lsum[:, :]))
                    dve.tensor_tensor(score[:, :, :], lexp[:, :, :], spread(lsum, 8), ALU.mult).then_inc(g_step, 1)
                elif piece in (1, 2):
                    dve.wait_ge(g_step, after(G_STEPS * batch + 6))
                    apart(dve)
                    for i in range((piece - 1) * NB // 2, piece * NB // 2):
                        dve.max(top8[:, i, :], score[:, i, :]).then_inc(g_step, 1)
                else:
                    dve.wait_ge(g_step, after(G_STEPS * batch + 6 + NB))
                    link(dve.tensor_reduce(tsum[:, :], top8[:, :, 0:2], AX.X, ALU.add))
                    link(dve.reciprocal(tsum[:, :], tsum[:, :]))
                    link(dve.tensor_tensor(wtop[:, :, :], top8[:, :, 0:2], spread(tsum, 2), ALU.mult))
                    link(dve.tensor_reduce(wsum[:, :], wtop[:, :, :], AX.X, ALU.add))

            def finish(kind, b, batch, i):
                if i == 0:
                    dve.wait_ge(x1b_ready, after(NB * batch + NB))
                tile_wait(dve, kind, b, ("ffn", i))
                bank = bank_of(kind, ("ffn", i))
                dve.scalar_tensor_tensor(out=y[:, i % 2, :], in0=bank[:, D:2 * D], scalar=wsum[:, i:i + 1],
                                         in1=x1[:, i, :], op0=ALU.mult, op1=ALU.add).then_inc(y_ready, 1)
                dve.wait_ge(y_ready, after(NB * batch + i + 1))
                dve.tensor_tensor(x1[:, i, :], bank[:, 0:D], y[:, i % 2, :], ALU.add).then_inc(tile_dve, 1)

            def silu_of_c():
                dve.wait_ge(c_exp, 1)
                dve.tensor_scalar(ect[:, :, :], ect[:, :, :], 1.0, None, ALU.add).then_inc(silu_step, 1)
                dve.wait_ge(silu_step, 1)
                dve.reciprocal(ect[:, :, :], ect[:, :, :]).then_inc(silu_step, 1)
                dve.wait_ge(silu_step, 2)
                dve.tensor_tensor(silu[:, :, :], ct[:, :, :], ect[:, :, :], ALU.mult).then_inc(silu_step, 1)

            def modulation():
                dve.wait_ge(mod_mm, 1)
                dve.tensor_copy(modc[:, :, :, :].rearrange("p m k b -> p (m k b)"),
                                ps_x[0][:, 0:6 * KT * B]).then_inc(mod_step, 1)
                dve.wait_ge(mod_step, 1)
                for m in (MOD_CA, MOD_CB):
                    dve.tensor_scalar(modc[:, m, :, :], modc[:, m, :, :], 1.0, None, ALU.add).then_inc(mod_step, 1)
                dve.wait_ge(mod_mm, 2)
                dve.tensor_copy(grow[:, :], ps_o[0:B, :]).then_inc(mod_step, 1)
                dve.wait_ge(mod_step, 4)
                dve.tensor_scalar(gsign, grow[:, :], 0.0, 2.0, ALU.is_ge, ALU.mult).then_inc(mod_step, 1)
                dve.scalar_tensor_tensor(out=gabs, in0=grow[:, :], scalar=-1.0, in1=grow[:, :],
                                         op0=ALU.mult, op1=ALU.max).then_inc(mod_step, 1)
                dve.wait_ge(mod_step, 6)
                dve.tensor_scalar(gabs, gabs, GATE_FLOOR, None, ALU.max).then_inc(mod_step, 1)
                dve.wait_ge(mod_step, 7)
                dve.scalar_tensor_tensor(out=grow[:, :], in0=gsign, scalar=-1.0, in1=gabs,
                                         op0=ALU.add, op1=ALU.mult).then_inc(gate_ready, 1)
                dve.memset(ps_o[:, :], 0.0).then_inc(gate_ready, 1)
                dve.wait_ge(w_loaded, 16 * N_WLOADS)

            def part(kind, b):
                nxt = 0 if kind == "start" else b + 1
                last = b - 1
                for what, *arg in plan_of(kind):
                    if what == "score":
                        maximum(kind, b, *arg)
                    elif what == "split_max":
                        split_maxima(kind, b, *arg)
                    elif what == "m":
                        maxima_rows(kind, b, *arg)
                    elif what == "modulation":
                        modulation()
                    elif what == "v":
                        values(kind, b, *arg)
                    elif what == "turn":
                        turn(kind, b, last if tuple(arg) == (NG - 1, NC - 1) else b, *arg)
                    elif what == "wo":
                        output(kind, b, last, *arg)
                    elif what == "aggregate":
                        aggregate(arg[0], last if arg[0] else nxt)
                    elif what == "normalise":
                        s, half = arg
                        normalise(kind, b, s, half, last if s else nxt, x1 if s else xs)
                    elif what == "stats":
                        i, = arg
                        if i == 0:
                            dve.wait_ge(x_loaded, after(16 * nxt + 16))
                        statistics(0, xs, i)
                    elif what == "gate":
                        take_logits(kind, b)
                    elif what == "gate_soft":
                        gate_softmax(kind, b, last)
                    elif what == "gate_top":
                        gate_top(last, *arg)
                    elif what == "ffn":
                        finish(kind, b, last, *arg)
                    elif what == "second_part":
                        second_part(nxt, *arg)

            dve.memset(v[:, :, :, DH:DH + 1], 1.0).then_inc(dve_const, 1)
            dve.memset(mpart[:, :, :, :], MASKED).then_inc(dve_const, 1)
            dve.memset(logit[:, :, :], MASKED).then_inc(dve_const, 1)
            for t in (0, 1):
                dve.memset(ks[t][ROWS:ROWS + MROWS, :, :], 1.0).then_inc(dve_const, 1)
            dve.wait_ge(dve_const, 5)
            silu_of_c()
            steps(dve, part)

        @block.tensor
        def _(pe):
            def claim(kind, b, tile):
                tiles = TILES[kind]
                banks = 4 if kind in ("start", "end") else 3
                n = tiles.index[tile]
                before = counts_before(kind, b)
                if n >= banks:
                    taken(kind, b, tiles.order[n - banks])
                elif n == 0 and kind not in ("start", "end"):
                    pe.wait_ge(tile_act, after(before[1]))
                    pe.wait_ge(tile_dve, after(before[2]))
                return bank_of(kind, tile)

            def taken(kind, b, tile):
                on_act, count = TILES[kind].taken(tile)
                before = counts_before(kind, b)
                pe.wait_ge(tile_act if on_act else tile_dve, after(before[1 if on_act else 2] + count))

            def values(kind, b, n):
                bank = claim(kind, b, ("v", n))
                for i in range(2):
                    blk = 2 * n + i
                    for k in range(KT):
                        mm = pe.matmul(bank[:, i * D:(i + 1) * D], ht[:, k, blk * P:(blk + 1) * P],
                                       wv[:, k, :], start=(k == 0), stop=(k == KT - 1))
                mm.then_inc(tile_mm, 1)

            def turn(kind, b, batch, t, c):
                bank = claim(kind, b, ("turn", t, c))
                pe.wait_ge(po_evac, after(NC * (NG * batch + t) + c + 1))
                for j in range(CH // P):
                    mm = pe.transpose(bank[:, j * P:(j + 1) * P], ot[:, c, j * P:(j + 1) * P], ident[:, :])
                mm.then_inc(tile_mm, 1)

            def features(kind, b, i):
                bank = claim(kind, b, ("on", i))
                if i == 0:
                    taken(kind, b, ("turn", NG - 1, NC - 1))
                for k in range(KT):
                    mm = pe.transpose(bank[:, k * P:(k + 1) * P],
                                      on[:, i, 8 * k:8 * k + 8, :].rearrange("p h d -> p (h d)"), ident[:, :])
                mm.then_inc(tile_mm, 1)

            def project_out(kind, b, batch, i):
                bank = claim(kind, b, ("wo", i))
                taken(kind, b, ("on", i))
                if i == 0:
                    pe.wait_ge(w_scaled, after(6 * batch + 6))
                for k in range(KT):
                    mm = pe.matmul(bank[:, 0:D], ont[:, i % 2, k, :], wo_g[:, k, :],
                                   start=(k == 0), stop=(k == KT - 1))
                mm.then_inc(tile_mm, 1)

            def transpose_h(kind, b, s, batch, i):
                bank = claim(kind, b, ("h", s, i))
                k, ch = i // 2, i % 2
                pe.wait_ge(xn_ready[s], after(NB * batch + 4 * ch + 4))
                for q in range(4):
                    mm = pe.transpose(bank[:, q * P:(q + 1) * P], xn[:, 4 * ch + q, k * P:(k + 1) * P], ident[:, :])
                mm.then_inc(tile_mm, 1)

            def gate_logits(kind, b):
                bank = claim(kind, b, ("gate",))
                taken(kind, b, ("h", 1, 3))
                for i in range(NB):
                    for k in range(KT):
                        mm = pe.matmul(bank[:, 8 * i:8 * i + E_GATE], ht[:, k, i * P:(i + 1) * P], wg[:, k, :],
                                       start=(k == 0), stop=(k == KT - 1))
                mm.then_inc(tile_mm, 1)

            def ffn(kind, b, i):
                bank = claim(kind, b, ("ffn", i))
                for k in range(KT):
                    mm = pe.matmul(bank, ht[:, k, i * P:(i + 1) * P], wse_g[:, k, :],
                                   start=(k == 0), stop=(k == KT - 1))
                mm.then_inc(tile_mm, 1)

            def project_qk(kind, b, n):
                mt, which, c = n // 4, n // 2 % 2, n % 2
                bank = claim(kind, b, ("qk", n))
                if n == 0:
                    taken(kind, b, ("h", 0, 3))
                for k in range(KT):
                    mm = pe.matmul(bank, (wq, wk)[which][:, k, mt * P:(mt + 1) * P],
                                   ht[:, k, c * CH:(c + 1) * CH], start=(k == 0), stop=(k == KT - 1))
                mm.then_inc(tile_mm, 1)

            def scores(kind, b, t, k):
                i, half, h0, heads, key0, keys = MAX_TILES[k]
                if k == 0:
                    batch = 0 if kind == "start" else b + 1 if t == 0 else b
                    pe.wait_ge(stack_loaded[t], after(192 * batch + 192))
                bank = claim(kind, b, ("score", t, k))
                for h in range(heads):
                    hh = h0 + h
                    o = bank[:, h * keys:(h + 1) * keys]
                    diagonal = key0 + keys == (i + 1) * P
                    mm = pe.matmul(o, qs[t][0:ROWS, hh, i * P:(i + 1) * P], ks[t][0:ROWS, hh, key0:key0 + keys],
                                   start=True, stop=not diagonal)
                    if diagonal:
                        mm = pe.matmul(o[:, keys - P:keys], ident_b[:, :], mask_b[:, :], start=False, stop=True)
                mm.then_inc(tile_mm, 1)

            def transpose_maxima(kind, b, t):
                bank = claim(kind, b, ("m", t))[:, 0:P // 2].bitcast(BF16)
                g = score_group(-1 if kind == "start" else b, t)
                pe.wait_ge(m3_ready, after(g + 1))
                pe.transpose(bank[0:MROWS * HG * NB, :], m3[:, :, :].rearrange("p r n -> p (r n)"),
                             ident_b[:, :]).then_inc(tile_mm, 1)

            def scores_t(kind, b, t, u, pr):
                c, j, first, width, diagonal = UNITS[u]
                if u == 0 and pr == 0:
                    pe.wait_ge(mrow_loaded[t], after(48 * b + 48))
                    if kind == "first" and t == 0:
                        taken("start", 0, ("qk", 7))
                        pe.wait_ge(pool_const, 11)
                        pe.wait_ge(gate_ready, 2)
                        taken("start", 0, ("m", 0))
                e = NEXP * t + 2 * u + pr
                if not (kind == "first" and e < 2):
                    pe.wait_ge(exp_done, after(NEXP * NG * b + e - 1))
                for h in range(2):
                    hh = 2 * pr + h
                    mm = pe.matmul(ps_t[pr][:, h, 0:width], ks[t][0:ROWS + MROWS, hh, j * P:(j + 1) * P],
                                   qs[t][0:ROWS + MROWS, hh, first:first + width], start=True, stop=True)
                mm.then_inc(st_mm, 1)

            def weigh_values(kind, b, t, u):
                c, j, first, width, diagonal = UNITS[u]
                last = u + 1 == NU or UNITS[u + 1][0] != c
                pe.wait_ge(exp_done, after(NEXP * (NG * b + t) + 2 * u + 2))
                if diagonal:
                    pe.wait_ge(diag_done, after(NDIAG * (NG * b + t) + sum(x[4] for x in UNITS[:u + 1])))
                if t == 0 and j % 2 == 0:
                    taken(kind, b, ("v", j // 2))
                if j == 0:
                    pe.wait_ge(po_evac, after(NC * (NG * b + t) + c))
                for hh in range(HG):
                    mm = pe.matmul(ps_o[32 * hh:32 * hh + DH + 1, CH - width:CH], v[:, j, HG * t + hh, :],
                                   probs[u % NP_BUF][:, hh, 0:width], start=(j == 0), stop=last)
                mm.then_inc(pv_done, 1)

            def modulation():
                pe.wait_ge(wm_loaded, 16)
                pe.wait_ge(silu_step, 3)
                for m in range(6 * KT):
                    for k in range(KT):
                        mm = pe.matmul(ps_x[0][:, m * B:(m + 1) * B], wm[:, k, m * P:(m + 1) * P], silu[:, k, :],
                                       start=(k == 0), stop=(k == KT - 1))
                mm.then_inc(mod_mm, 1)
                for e, m in enumerate((MOD_GA, MOD_GB)):
                    for k in range(KT):
                        mm = pe.matmul(ps_o[0:B, e * D:(e + 1) * D], silu[:, k, :], wm[:, k, m * D:(m + 1) * D],
                                       start=(k == 0), stop=(k == KT - 1))
                mm.then_inc(mod_mm, 1)
                pe.wait_ge(w_loaded, 16 * N_WLOADS)

            def spread_gates(kind, b, batch):
                bank = claim(kind, b, ("bc", batch))
                pe.wait_ge(gate_ready, 1)
                pe.matmul(bank, sel[:, batch, :], grow[:, :], start=True, stop=True).then_inc(tile_mm, 1)

            def part(kind, b):
                nxt = 0 if kind == "start" else b + 1
                last = b - 1
                for what, *arg in plan_of(kind):
                    if what == "modulation":
                        modulation()
                    elif what == "bc":
                        spread_gates(kind, b, *arg)
                    elif what == "attend":
                        scores_t(kind, b, *arg)
                    elif what == "weigh":
                        weigh_values(kind, b, *arg)
                    elif what == "score":
                        scores(kind, b, *arg)
                    elif what == "m":
                        transpose_maxima(kind, b, *arg)
                    elif what == "v":
                        values(kind, b, *arg)
                    elif what == "turn":
                        turn(kind, b, last if tuple(arg) == (NG - 1, NC - 1) else b, *arg)
                    elif what == "on":
                        features(kind, b, *arg)
                    elif what == "wo":
                        project_out(kind, b, last, *arg)
                    elif what == "h":
                        s, i = arg
                        transpose_h(kind, b, s, last if s else nxt, i)
                    elif what == "gate":
                        gate_logits(kind, b)
                    elif what == "ffn":
                        ffn(kind, b, *arg)
                    elif what == "qk":
                        project_qk(kind, b, *arg)

            pe.wait_ge(pool_const, 9)
            steps(pe, part)


def kernel(L0_attn_x, L0_attn_Wq_w, L0_attn_Wq_b, L0_attn_Wk_w, L0_attn_Wk_b, L0_attn_Wv_w, L0_attn_Wv_b,
           L0_attn_Wo_w, L0_attn_Wo_b, L0_ffn_cond, L0_ffn_mask, L0_ffn_W_shared, L0_ffn_W_expert,
           L0_ffn_W_gate, L0_ffn_bias, L0_c, L0_wmod):
    import numpy as np
    import concourse.bacc as bacc
    from concourse.bass_utils import run_bass_kernel_spmd

    def rows(a):
        return np.ascontiguousarray(a)

    def turned(a):
        return np.ascontiguousarray(np.asarray(a).T)

    def line(a):
        return rows(a).reshape(1, -1)

    arrays = {
        "x": rows(L0_attn_x), "wq_t": turned(L0_attn_Wq_w), "wk_t": turned(L0_attn_Wk_w),
        "wv_t": turned(L0_attn_Wv_w), "wo_t": turned(L0_attn_Wo_w), "ws_t": turned(L0_ffn_W_shared),
        "we_t": turned(L0_ffn_W_expert), "wgate": rows(L0_ffn_W_gate),
        "bq": turned(rows(L0_attn_Wq_b).reshape(KT, P)), "bk": turned(rows(L0_attn_Wk_b).reshape(KT, P)),
        "bv": line(L0_attn_Wv_b), "bo": line(L0_attn_Wo_b), "bf": line(L0_ffn_bias),
        "c_t": turned(L0_c), "wmod": rows(L0_wmod),
    }
    nc = bacc.Bacc("TRN2", target_bir_lowering=False, num_devices=1)
    args = {n: nc.dram_tensor(n, a.shape, mybir.dt.from_np(a.dtype), kind="ExternalInput").ap()
            for n, a in arrays.items()}
    args["out"] = nc.dram_tensor("out", (B, T, D), F32, kind="ExternalOutput").ap()
    adaln_block(nc, **args)
    r = run_bass_kernel_spmd(nc, [arrays], core_ids=[0])
    return r.results[0]["out"]
```
